# Optimizing a Trainium2 kernel written in Bass

```python
import numpy as np
import jax
import jax.numpy as jnp

def _softmax(x, axis=-1):
    return jax.nn.softmax(x, axis=axis)

def _gelu(x):
    return jax.nn.gelu(x, approximate=True)

def _silu(x):
    return jax.nn.silu(x)

def _sigmoid(x):
    return jax.nn.sigmoid(x)

def _layernorm(x, axis=-1, eps=1e-05):
    m = jnp.mean(x, axis=axis, keepdims=True)
    v = jnp.var(x, axis=axis, keepdims=True)
    return (x - m) / jnp.sqrt(v + eps)

def _scatter_add(tgt, idx, src, axis=0):
    return tgt.at[idx].add(src)

def _segment_sum(src, seg, n):
    return jax.ops.segment_sum(src, seg, n)
kernel_name = 'mk_xattn_seq_d1_seqx_r2_e184a8'

def setup_inputs(seed: int=0):
    np.random.seed(seed)
    _w = jnp.asarray

    def _rec_inputs():
        import jax
        import jax.numpy as jnp
        _rk = jax.random.key(seed)
        x = -0.0001108 + 0.9999 * jax.random.normal(jax.random.fold_in(_rk, 1), (2, 2048, 640), jnp.float32)
        _lenS = 2048 - jax.random.randint(jax.random.fold_in(_rk, 7), (2,), 0, max(1, 2048 // 4) + 1, jnp.int32)
        _lenS2 = 154 - jax.random.randint(jax.random.fold_in(_rk, 8), (2,), 0, max(1, 154 // 4) + 1, jnp.int32)
        _ctx_2048P = jax.random.normal(jax.random.fold_in(_rk, 11), (2, 16, 1024), jnp.float32)
        _ctx_2048c = jax.random.dirichlet(jax.random.fold_in(_rk, 511), 0.3 * jnp.ones((16,), jnp.float32), (2, 154))
        _ctx_2048t = jnp.einsum('bsk,bkd->bsd', _ctx_2048c, _ctx_2048P)
        _ctx_2048t = _ctx_2048t * jax.lax.rsqrt(jnp.mean(jnp.square(_ctx_2048t)) + 1e-12) * 0.953939
        ctx_2048 = -0.000395056 + 1.00006 * (_ctx_2048t + 0.3 * jax.random.normal(jax.random.fold_in(_rk, 611), (2, 154, 1024), jnp.float32))
        return (x, ctx_2048)
    x, ctx_2048 = _rec_inputs()

    def _L0_xattn_setup():
        import jax, jax.numpy as jnp
        import numpy as np
        NUM_HEADS = 20
        TEXT_LEN = 77
        IP_SCALE = 1.0

        def _attend(q, k, v, sm_scale):
            scores = jnp.einsum('bhsd,bhld->bhsl', q, k) * sm_scale
            probs = jax.nn.softmax(scores, axis=-1)
            return jnp.einsum('bhsl,bhld->bhsd', probs, v)

        def _split_heads(x, h):
            b, s, c = x.shape
            return x.reshape(b, s, h, c // h).transpose(0, 2, 1, 3)

        def _merge_heads(x):
            b, h, s, d = x.shape
            return x.transpose(0, 2, 1, 3).reshape(b, s, h * d)
        key = jax.random.key(seed)
        ks = jax.random.split(key, 8)
        B, S, C, CC, L = (8, 2048, 640, 1024, TEXT_LEN + 4)
        sd_q = 1.0 / np.sqrt(C)
        sd_kv = 1.0 / np.sqrt(CC)
        return {'hidden_states': jax.random.normal(ks[0], (B, S, C), jnp.float32), 'encoder_hidden_states': jax.random.normal(ks[1], (B, L, CC), jnp.float32), 'Wq': jax.random.normal(ks[2], (C, C), jnp.float32) * sd_q, 'Wk': jax.random.normal(ks[3], (C, CC), jnp.float32) * sd_kv, 'Wv': jax.random.normal(ks[4], (C, CC), jnp.float32) * sd_kv, 'Wk_ip': jax.random.normal(ks[5], (C, CC), jnp.float32) * sd_kv, 'Wv_ip': jax.random.normal(ks[6], (C, CC), jnp.float32) * sd_kv, 'Wo': jax.random.normal(ks[7], (C, C), jnp.float32) * sd_q, 'bo': jnp.zeros((C,), jnp.float32)}
    _L0_xattn_all = _L0_xattn_setup()
    _L0_xattn_in = {k: v for k, v in _L0_xattn_all.items() if k in ('Wq', 'Wk', 'Wv', 'Wk_ip', 'Wv_ip', 'Wo', 'bo')}
    del _L0_xattn_all
    return {'x': x, 'ctx_2048': ctx_2048, 'L0_xattn_Wq': _L0_xattn_in['Wq'], 'L0_xattn_Wk': _L0_xattn_in['Wk'], 'L0_xattn_Wv': _L0_xattn_in['Wv'], 'L0_xattn_Wk_ip': _L0_xattn_in['Wk_ip'], 'L0_xattn_Wv_ip': _L0_xattn_in['Wv_ip'], 'L0_xattn_Wo': _L0_xattn_in['Wo'], 'L0_xattn_bo': _L0_xattn_in['bo']}

def reference(x, ctx_2048, L0_xattn_Wq, L0_xattn_Wk, L0_xattn_Wv, L0_xattn_Wk_ip, L0_xattn_Wv_ip, L0_xattn_Wo, L0_xattn_bo):
    import jax
    import jax.numpy as jnp

    def _L0_xattn_ref(hidden_states, encoder_hidden_states, Wq, Wk, Wv, Wk_ip, Wv_ip, Wo, bo):
        import jax, jax.numpy as jnp
        import numpy as np
        NUM_HEADS = 20
        TEXT_LEN = 77
        IP_SCALE = 1.0

        def _attend(q, k, v, sm_scale):
            scores = jnp.einsum('bhsd,bhld->bhsl', q, k) * sm_scale
            probs = jax.nn.softmax(scores, axis=-1)
            return jnp.einsum('bhsl,bhld->bhsd', probs, v)

        def _split_heads(x, h):
            b, s, c = x.shape
            return x.reshape(b, s, h, c // h).transpose(0, 2, 1, 3)

        def _merge_heads(x):
            b, h, s, d = x.shape
            return x.transpose(0, 2, 1, 3).reshape(b, s, h * d)
        residual = hidden_states
        B, S, C = hidden_states.shape
        H = NUM_HEADS
        D = C // H
        sm_scale = 1.0 / jnp.sqrt(jnp.asarray(D, hidden_states.dtype))
        text = encoder_hidden_states[:, :TEXT_LEN, :]
        ip = encoder_hidden_states[:, TEXT_LEN:, :]
        q = _split_heads(hidden_states @ Wq.T, H)
        k = _split_heads(text @ Wk.T, H)
        v = _split_heads(text @ Wv.T, H)
        out_text = _merge_heads(_attend(q, k, v, sm_scale))
        k_ip = _split_heads(ip @ Wk_ip.T, H)
        v_ip = _split_heads(ip @ Wv_ip.T, H)
        out_ip = _merge_heads(_attend(q, k_ip, v_ip, sm_scale))
        out = out_text + IP_SCALE * out_ip
        out = out @ Wo.T + bo
        return out + residual
    x = _L0_xattn_ref(x, ctx_2048, L0_xattn_Wq, L0_xattn_Wk, L0_xattn_Wv, L0_xattn_Wk_ip, L0_xattn_Wv_ip, L0_xattn_Wo, L0_xattn_bo)
    return x

_drawn_inputs = setup_inputs


def setup_inputs(seed=0):
    import zlib

    import numpy as np

    out = dict(_drawn_inputs(seed))
    spreads = {'L0_xattn_bo': (0.0, 0.1)}
    factors = {}
    for name, (base, spread) in spreads.items():
        noise = np.random.default_rng([zlib.crc32(name.encode()), seed]).standard_normal(out[name].shape)
        drawn = base * np.exp(spread * noise) if base else spread * noise
        out[name] = jnp.asarray(drawn.astype(out[name].dtype))
    for name, factor in factors.items():
        out[name] = (out[name] * factor).astype(out[name].dtype)
    return out
```

```python
from contextlib import ExitStack

import numpy as np

import concourse.bass as bass
from concourse import mybir

ACT = mybir.ActivationFunctionType
ALU = mybir.AluOpType
AXIS = mybir.AxisListType
F32 = mybir.dt.float32
F32R = mybir.dt.float32r

P = 128
BATCHES, SEQ, C, CTX_C = 2, 2048, 640, 1024
HEADS, KEYS, BRANCHES = 20, 77, 2
D = C // HEADS
SCALE = float(np.float32(1.0) / np.sqrt(np.float32(D)))
GROUP = P // D
GROUPS = C // P
CTX_CHUNKS = CTX_C // P
N = 256
SUB = N // P
TILES = BATCHES * SEQ // N
STEPS = TILES // BATCHES
UNITS = TILES * GROUPS
BLK = GROUP * KEYS
SHIFT_ROW = 3 * D
STACK = SHIFT_ROW + BRANCHES
MAXES = SUB * BRANCHES
A_ITEMS = MAXES + 1
X_ITEMS = 2 * GROUPS
V_COLS = C // 2
DMA = 16


class Unit:

    def __init__(self, t, c):
        carry, c = divmod(c, GROUPS * BATCHES)
        self.t, self.c = t + carry, c
        self.batch, self.g = divmod(c, GROUPS)
        self.slot = c % 2
        self.fixed = isinstance(self.t, int)

    def plus(self, k):
        return Unit(self.t, self.c + k)

    def tile_plus(self, k):
        return Unit(self.t, self.c - self.g + k * GROUPS)

    def number(self, scale=1, plus=0):
        return self.t * (GROUPS * BATCHES * scale) + (self.c * scale + plus)

    def tile(self, scale=1, plus=0):
        return self.t * (BATCHES * scale) + (self.batch * scale + plus)

    def uses_of_slot(self, scale=1):
        return self.t * (GROUPS * BATCHES // 2 * scale) + (self.c // 2 + 1) * scale

    def exists(self):
        return not self.fixed or 0 <= self.t < STEPS


def wait(eng, sem, value):
    if not isinstance(value, int) or value > 0:
        eng.wait_ge(sem, value)


def build(nc, x_d, ctx_d, wq_d, wk_d, wv_d, wo_d, bo_d, out_d):
    with ExitStack() as stack:
        def sbuf(name, shape, dt=F32, scope=stack):
            return scope.enter_context(nc.sbuf_tensor(name, shape, dt))

        def psum(name):
            return stack.enter_context(nc.psum_tensor(name, [P, 512], F32))

        def sem(name):
            return stack.enter_context(nc.semaphore(name))

        wq_hi = sbuf("wq_hi", [P, GROUPS, C], F32R)
        wq_lo = sbuf("wq_lo", [P, GROUPS, C], F32R)
        wo_hi = sbuf("wo_hi", [P, GROUPS, C], F32R)
        wo_lo = sbuf("wo_lo", [P, GROUPS, C], F32R)
        k_stack = sbuf("k_stack", [P, BRANCHES, HEADS, BATCHES, KEYS], F32R)
        k_diag = sbuf("k_diag", [P, BRANCHES, GROUPS, BATCHES, GROUP, KEYS], F32R)
        v = sbuf("v", [P, BRANCHES, BATCHES, C])
        bo = sbuf("bo", [P, GROUPS])
        ident = sbuf("ident", [P, P])
        sum_first = sbuf("sum_first", [P, D])
        sum_one = sbuf("sum_one", [P, 2 * D])
        spread = sbuf("spread", [P, BRANCHES * GROUPS, GROUP, D], F32R)
        x_raw = sbuf("x_raw", [P, GROUPS, N])
        x_hi = sbuf("x_hi", [P, BATCHES, GROUPS, N], F32R)
        x_lo = sbuf("x_lo", [P, BATCHES, GROUPS, N], F32R)
        q_hi = sbuf("q_hi", [P, 2, N], F32R)
        q_stack = sbuf("q_stack", [P, 2, GROUP, N], F32R)
        row_max = sbuf("row_max", [P, 2, SUB, BRANCHES * GROUP])
        max_rows = sbuf("max_rows", [BRANCHES * GROUP, 2, N], F32R)
        stage = [sbuf(f"stage{i}", [P, CTX_CHUNKS * C]) for i in range(2)]
        probs = stage[0][:, 0:GROUP * BRANCHES * N].rearrange("p (j n) -> p j n", j=GROUP)
        scaled = stage[0][:, GROUP * BRANCHES * N:][:, 0:2 * BRANCHES * N].rearrange("p (s n) -> p s n", s=2)
        pv_sb = stage[1][:, 0:GROUPS * BRANCHES * N].rearrange("p (g n) -> p g n", g=GROUPS)
        attn = stage[1][:, GROUPS * BRANCHES * N:][:, 0:GROUPS * N].rearrange("p (g n) -> p g n", g=GROUPS)
        res = stage[1][:, GROUPS * (BRANCHES + 1) * N:][:, 0:GROUPS * N].rearrange("p (g n) -> p g n", g=GROUPS)
        with ExitStack() as before:
            ctx = sbuf("ctx", [P, CTX_CHUNKS, BRANCHES, BATCHES, KEYS], scope=before)
        attn_hi = sbuf("attn_hi", [P, GROUPS, N], F32R)
        attn_lo = sbuf("attn_lo", [P, GROUPS, N], F32R)
        inv = sbuf("inv", [P, N])
        inv_hi = sbuf("inv_hi", [P, N], F32R)
        inv_lo = sbuf("inv_lo", [P, N], F32R)

        q_ps = psum("q_ps")
        x_ps = psum("x_ps")
        a_ps = [psum("a_ps0"), psum("a_ps1")]
        b_ps = [psum("b_ps0"), psum("b_ps1")]
        pv_ps = psum("pv_ps")
        sum_ps = psum("sum_ps")

        x_loaded = sem("x_loaded")
        wq_loaded = sem("wq_loaded")
        ctx_loaded = sem("ctx_loaded")
        bo_loaded = sem("bo_loaded")
        wk_loaded = [sem(f"wk_loaded{br}") for br in range(BRANCHES)]
        wv_loaded = [sem(f"wv_loaded{br}") for br in range(BRANCHES)]
        wo_loaded = sem("wo_loaded")
        wq_hi_done, wq_lo_done = sem("wq_hi_done"), sem("wq_lo_done")
        wo_hi_done, wo_lo_done = sem("wo_hi_done"), sem("wo_lo_done")
        zeroed = sem("zeroed")
        consts = sem("consts")
        shift_done = sem("shift_done")
        k_acc = sem("k_acc")
        k_hi_done = sem("k_hi_done")
        k_lo_done = sem("k_lo_done")
        k_copied = sem("k_copied")
        v_acc = sem("v_acc")
        v_done = [sem(f"v_done{half}") for half in range(2)]
        v_zeroed = sem("v_zeroed")
        probs_zeroed = sem("probs_zeroed")
        x_hi_done, x_lo_done = sem("x_hi_done"), sem("x_lo_done")
        q_acc = sem("q_acc")
        q_hi_done = sem("q_hi_done")
        q_top_done = sem("q_top_done")
        q_low_done = sem("q_low_done")
        a_ready, a_drained = sem("a_ready"), sem("a_drained")
        max_in = [sem(f"max_in{s}") for s in range(2)]
        b_ready, b_drained = sem("b_ready"), sem("b_drained")
        pv_ready = sem("pv_ready")
        pv_drained = sem("pv_drained")
        inv_done = sem("inv_done")
        x_ready, x_drained = sem("x_ready"), sem("x_drained")
        attn_done = sem("attn_done")
        attn_hi_done, attn_lo_done = sem("attn_hi_done"), sem("attn_lo_done")
        res_loaded = sem("res_loaded")
        stored = sem("stored")

        INV_STEPS = 3
        K_ITEMS = BRANCHES * GROUPS
        V_ITEMS = BRANCHES * BATCHES * (C // V_COLS)
        block = stack.enter_context(nc.Block())

        def stages(emit):
            def pair(t):
                for c in range(GROUPS * BATCHES):
                    emit(Unit(t, c))
            pair(0)
            with emit.engine.Fori(1, STEPS - 1) as t:
                pair(t)
            pair(STEPS - 1)
            for c in range(GROUPS):
                emit(Unit(STEPS, c))

        @block.sync
        def _(sp):
            sp.dma_start(x_raw[:], x_d[0, 0]).then_inc(x_loaded, DMA)
            sp.dma_start(stage[0][:, 0:GROUPS * C], wq_d).then_inc(wq_loaded, DMA)
            sp.dma_start(ctx[:], ctx_d).then_inc(ctx_loaded, DMA)
            sp.dma_start(stage[1][:], wk_d[0]).then_inc(wk_loaded[0], DMA)
            sp.dma_start(bo[:], bo_d).then_inc(bo_loaded, DMA)
            sp.wait_ge(wq_hi_done, 1)
            sp.wait_ge(wq_lo_done, 1)
            sp.dma_start(stage[0][:], wk_d[1]).then_inc(wk_loaded[1], DMA)
            sp.wait_ge(x_hi_done, 1)
            sp.wait_ge(x_lo_done, 1)
            sp.dma_start(x_raw[:], x_d[0, 1]).then_inc(x_loaded, DMA)
            sp.wait_ge(k_acc, GROUPS)
            sp.dma_start(stage[1][:], wv_d[0]).then_inc(wv_loaded[0], DMA)
            sp.wait_ge(k_acc, K_ITEMS)
            sp.dma_start(stage[0][:], wv_d[1]).then_inc(wv_loaded[1], DMA)
            sp.wait_ge(v_acc, V_ITEMS // 2)
            sp.dma_start(stage[1][:, 0:GROUPS * C], wo_d).then_inc(wo_loaded, DMA)

            def maxima(u):
                wait(sp, a_drained, u.number(A_ITEMS, A_ITEMS))
                for br in range(BRANCHES):
                    sp.dma_start(q_stack[SHIFT_ROW + br:SHIFT_ROW + br + 1, u.slot].bitcast(F32),
                                 max_rows[br * GROUP:(br + 1) * GROUP, u.slot, :].bitcast(F32)).then_inc(max_in[u.slot], DMA)

            def store(u, m):
                wait(sp, x_drained, u.tile(X_ITEMS, GROUPS + m + 1))
                sp.dma_start(out_d[u.t, u.batch, :, m, :], res[:, m, :]).then_inc(stored, DMA)

            def emit(u):
                before, ahead = u.tile_plus(-1), u.tile_plus(2)
                if u.g == 0 and u.tile_plus(-2).exists():
                    for m in range(GROUPS - 2, GROUPS):
                        store(u.tile_plus(-2), m)
                if u.g == 1:
                    if before.exists():
                        wait(sp, stored, before.tile(GROUPS * DMA))
                        if before.fixed and before.number() == 0:
                            sp.wait_ge(wo_hi_done, 1)
                            sp.wait_ge(wo_lo_done, 1)
                        sp.dma_start(res[:], x_d[before.t, before.batch]).then_inc(res_loaded, DMA)
                    if ahead.exists() and u.exists():
                        wait(sp, x_lo_done, u.tile(1, 2))
                        sp.dma_start(x_raw[:], x_d[ahead.t, ahead.batch]).then_inc(x_loaded, DMA)
                if u.g >= 2 and before.exists():
                    store(before, u.g - 2)
                if u.exists() and u.plus(1).exists():
                    maxima(u.plus(1))

            maxima(Unit(0, 0))
            emit.engine = sp
            stages(emit)
            last = Unit(STEPS - 1, GROUPS)
            for m in range(GROUPS - 2, GROUPS):
                store(last, m)
            sp.wait_ge(stored, TILES * GROUPS * DMA)

        @block.gpsimd
        def _(pool):
            nc.gpsimd.memset(ident[:], 0.0).then_inc(consts, 1)
            pool.wait_ge(consts, 1)
            nc.gpsimd.affine_select(out=ident[:], in_=ident[:], compare_op=ALU.not_equal, fill=1.0, base=0,
                                    pattern=[[-1, P]], channel_multiplier=1).then_inc(consts, 1)
            nc.gpsimd.memset(sum_one[:], 0.0).then_inc(consts, 1)
            nc.gpsimd.memset(sum_first[:], 1.0).then_inc(consts, 1)
            pool.wait_ge(consts, 4)
            nc.gpsimd.memset(sum_one[:, D - 1:D], 1.0).then_inc(consts, 1)
            nc.gpsimd.memset(sum_first[:, 1:BRANCHES * GROUPS], 0.0).then_inc(consts, 1)
            nc.gpsimd.memset(k_diag[:, 1].bitcast(F32), 0.0).then_inc(zeroed, 1)
            nc.gpsimd.memset(spread[:].bitcast(F32), 0.0).then_inc(consts, 1)
            pool.wait_ge(consts, 7)
            nc.gpsimd.affine_select(out=spread[:], in_=spread[:], compare_op=ALU.not_equal, fill=1.0, base=0,
                                    pattern=[[-1, BRANCHES * GROUPS], [-D, GROUP], [0, D]],
                                    channel_multiplier=1).then_inc(consts, 1)

            def split_x(u):
                wait(pool, x_hi_done, u.tile(1, 1))
                nc.gpsimd.tensor_tensor(x_lo[:, u.batch], x_raw[:], x_hi[:, u.batch].bitcast(F32),
                                        ALU.subtract).then_inc(x_lo_done, 1)

            def add_branches(u):
                n = u.tile(X_ITEMS, u.g + 1)
                wait(pool, x_drained, n)
                s = u.slot
                nc.gpsimd.tensor_tensor(attn[:, u.g, :], scaled[:, s, 0:N], scaled[:, s, N:2 * N],
                                        ALU.add).then_inc(attn_done, 1)

            def attn_low(u):
                wait(pool, attn_hi_done, u.number(1, 1))
                nc.gpsimd.tensor_tensor(attn_lo[:, u.g, :], attn[:, u.g, :], attn_hi[:, u.g, :].bitcast(F32),
                                        ALU.subtract).then_inc(attn_lo_done, 1)

            def emit(u):
                before, ahead = u.tile_plus(-1), u.tile_plus(1)
                if u.g == 0 and before.exists():
                    for g in range(GROUPS):
                        add_branches(before.plus(g))
                        if g:
                            attn_low(before.plus(g - 1))
                    attn_low(before.plus(GROUPS - 1))
                if u.g == 1 and ahead.exists():
                    split_x(ahead)

            split_x(Unit(0, 0))
            emit.engine = pool
            stages(emit)

        @block.scalar
        def _(act):
            act.wait_ge(x_loaded, DMA)
            nc.scalar.activation(x_hi[:, 0], x_raw[:], ACT.Copy).then_inc(x_hi_done, 1)
            act.wait_ge(wq_loaded, DMA)
            nc.scalar.activation(wq_hi[:], stage[0][:, 0:GROUPS * C].rearrange("p (k c) -> p k c", k=GROUPS),
                                 ACT.Copy).then_inc(wq_hi_done, 1)

            def q_high(u):
                wait(act, q_acc, u.number(1, 1))
                wait(act, a_ready, u.number(A_ITEMS, -A_ITEMS))
                nc.scalar.activation(q_hi[:, u.slot, :], q_ps[:, 0:N], ACT.Copy).then_inc(q_hi_done, 1)

            def q_top(u, heads):
                wait(act, b_ready, u.number(GROUP, -GROUP))
                wait(act, q_hi_done, u.number(1, 1))
                for j in heads:
                    done = nc.scalar.activation(q_stack[0:D, u.slot, j, :],
                                                q_hi[j * D:(j + 1) * D, u.slot, :].bitcast(F32), ACT.Copy)
                    if j == GROUP - 1:
                        done.then_inc(q_top_done, 1)

            def exp(u, j):
                wait(act, b_ready, u.number(GROUP, j + 1))
                if j == 0:
                    wait(act, pv_ready, u.number())
                nc.scalar.activation(probs[0:KEYS, j, :], b_ps[j % 2][0:KEYS, :], ACT.Exp).then_inc(b_drained, 1)

            def keep_pv(u):
                wait(act, pv_ready, u.number(1, 1))
                wait(act, x_drained, u.tile(X_ITEMS, u.g + 1 - X_ITEMS))
                nc.scalar.activation(pv_sb[:, u.g, :], pv_ps[:], ACT.Copy).then_inc(pv_drained, 1)

            def split_x(u):
                wait(act, x_loaded, u.tile(DMA, DMA))
                wait(act, q_acc, u.number(1, -GROUPS))
                nc.scalar.activation(x_hi[:, u.batch], x_raw[:], ACT.Copy).then_inc(x_hi_done, 1)

            def attn_high(u):
                wait(act, attn_done, u.number(1, 1))
                nc.scalar.activation(attn_hi[:, u.g, :], attn[:, u.g, :], ACT.Copy).then_inc(attn_hi_done, 1)

            def emit(u):
                before, ahead, nxt = u.tile_plus(-1), u.tile_plus(1), u.plus(1)
                move_q = u.exists() and nxt.exists()
                if move_q:
                    q_high(nxt)
                if u.exists():
                    exp(u, 0)
                    exp(u, 1)
                if move_q:
                    q_top(nxt, range(0, 2))
                if u.exists():
                    exp(u, 2)
                if move_q:
                    q_top(nxt, range(2, GROUP))
                if u.exists():
                    exp(u, 3)
                ends = u.g == 0 and before.exists()
                if ends:
                    attn_high(before)
                    attn_high(before.plus(1))
                if u.exists():
                    keep_pv(u)
                if ends:
                    for g in range(2, GROUPS):
                        attn_high(before.plus(g))
                if u.g == 1 and ahead.exists():
                    split_x(ahead)

            act.wait_ge(zeroed, 2)
            for item in range(K_ITEMS):
                br, g = divmod(item, GROUPS)
                act.wait_ge(k_acc, item + 1)
                for j in range(GROUP):
                    rows = slice(j * D, (j + 1) * D)
                    done = nc.scalar.activation(
                        k_diag[rows, br, g, :, j, :],
                        a_ps[item % 2][rows, 0:BATCHES * KEYS].rearrange("p (b n) -> p b n", b=BATCHES),
                        ACT.Copy, scale=SCALE)
                done.then_inc(k_hi_done, 1)
                act.wait_ge(k_hi_done, item + 1)
                for j in range(GROUP):
                    nc.scalar.activation(k_stack[0:D, br, g * GROUP + j], k_diag[j * D:(j + 1) * D, br, g, :, j, :].bitcast(F32),
                                         ACT.Copy).then_inc(k_copied, 1)
                if item == 0:
                    q_high(Unit(0, 0))
                    q_top(Unit(0, 0), range(GROUP))
            act.wait_ge(v_zeroed, 1)
            for item in range(0, V_ITEMS, 2):
                br, b, half = item // 4, item // 2 % 2, item % 2
                act.wait_ge(v_acc, item + 1)
                nc.scalar.activation(v[0:KEYS, br, b, half * V_COLS:(half + 1) * V_COLS],
                                     b_ps[half][0:KEYS, 0:V_COLS], ACT.Copy).then_inc(v_done[half], 1)
            act.wait_ge(wo_loaded, DMA)
            nc.scalar.activation(wo_hi[:], stage[1][:, 0:GROUPS * C].rearrange("p (k c) -> p k c", k=GROUPS),
                                 ACT.Copy).then_inc(wo_hi_done, 1)
            act.wait_ge(probs_zeroed, 1)
            act.wait_ge(wo_lo_done, 1)
            emit.engine = act
            stages(emit)

        @block.vector
        def _(dve):
            nc.vector.memset(k_diag[:, 0].bitcast(F32), 0.0).then_inc(zeroed, 1)
            nc.vector.memset(k_stack[SHIFT_ROW:STACK].bitcast(F32), 1.0).then_inc(shift_done, 1)
            nc.vector.memset(v[64:P], 0.0).then_inc(v_zeroed, 1)
            dve.wait_ge(wq_hi_done, 1)
            nc.vector.tensor_tensor(wq_lo[:], stage[0][:, 0:GROUPS * C].rearrange("p (k c) -> p k c", k=GROUPS),
                                    wq_hi[:].bitcast(F32), ALU.subtract).then_inc(wq_lo_done, 1)
            dve.wait_ge(consts, 2)
            dve.wait_ge(shift_done, 1)
            for br in range(BRANCHES):
                pick = ident[SHIFT_ROW:STACK, SHIFT_ROW + br:SHIFT_ROW + br + 1]
                nc.vector.tensor_scalar(k_stack[SHIFT_ROW:STACK, br], k_stack[SHIFT_ROW:STACK, br].bitcast(F32),
                                        pick, -1.0, ALU.mult, ALU.mult).then_inc(shift_done, 1)

            def q_low(u, heads):
                wait(dve, q_hi_done, u.number(1, 1))
                wait(dve, b_ready, u.number(GROUP, -GROUP))
                for j in heads:
                    rows = slice(j * D, (j + 1) * D)
                    nc.vector.tensor_tensor(q_stack[D:2 * D, u.slot, j, :], q_ps[rows, 0:N],
                                            q_hi[rows, u.slot, :].bitcast(F32), ALU.subtract)
                    done = nc.vector.tensor_copy(q_stack[2 * D:3 * D, u.slot, j, :], q_hi[rows, u.slot, :].bitcast(F32))
                    if j == GROUP - 1:
                        done.then_inc(q_low_done, 1)

            def max_piece(u, k):
                item = u.number(A_ITEMS, k)
                sub, br = divmod(k, BRANCHES)
                wait(dve, a_ready, u.number(A_ITEMS, k + 1))
                bank = a_ps[(u.c * A_ITEMS + k) % 2]
                nc.vector.tensor_reduce(row_max[:, u.slot, sub, br * GROUP:(br + 1) * GROUP],
                                        bank[:, 0:BLK].rearrange("p (j n) -> p j n", j=GROUP), AXIS.X,
                                        ALU.max).then_inc(a_drained, 1)

            def max_turned(u):
                wait(dve, a_ready, u.number(A_ITEMS, A_ITEMS))
                wait(dve, max_in[u.slot], u.uses_of_slot(BRANCHES * DMA) - BRANCHES * DMA)
                nc.vector.tensor_copy(max_rows[:, u.slot, :],
                                      a_ps[(u.c * A_ITEMS + MAXES) % 2][0:BRANCHES * GROUP, 0:N]).then_inc(a_drained, 1)

            def invert_sums(u):
                wait(dve, pv_ready, u.number(1, 1))
                wait(dve, x_ready, u.tile(X_ITEMS, GROUPS - X_ITEMS))
                nc.vector.reciprocal(inv[:], sum_ps[:, 0:N]).then_inc(inv_done, 1)
                wait(dve, inv_done, u.tile(INV_STEPS, 1))
                nc.vector.tensor_copy(inv_hi[:], inv[:]).then_inc(inv_done, 1)
                wait(dve, inv_done, u.tile(INV_STEPS, 2))
                nc.vector.tensor_tensor(inv_lo[:], inv[:], inv_hi[:].bitcast(F32), ALU.subtract).then_inc(inv_done, 1)

            def normalise(u):
                wait(dve, x_ready, u.tile(X_ITEMS, u.g + 1))
                wait(dve, pv_drained, u.number(1, 1))
                wait(dve, attn_done, u.number(1, -1))
                nc.vector.tensor_tensor(scaled[:, u.slot, :], x_ps[:], pv_sb[:, u.g, :],
                                        ALU.mult).then_inc(x_drained, 1)

            def finish(u, m):
                wait(dve, x_ready, u.tile(X_ITEMS, GROUPS + m + 1))
                if m == 0:
                    wait(dve, res_loaded, u.tile(DMA, DMA))
                nc.vector.scalar_tensor_tensor(out=res[:, m, :], in0=x_ps[:, 0:N], scalar=bo[:, m:m + 1],
                                               in1=res[:, m, :], op0=ALU.add, op1=ALU.add).then_inc(x_drained, 1)

            def emit(u):
                before, nxt = u.tile_plus(-1), u.plus(1)
                drains = []
                if before.exists():
                    if u.g == 0:
                        drains = [lambda g=g: normalise(before.plus(g)) for g in range(GROUPS)]
                    elif u.g < GROUPS - 1:
                        drains = [lambda: finish(before, u.g - 1)]
                    else:
                        drains = [lambda m=m: finish(before, m) for m in range(GROUPS - 2, GROUPS)]
                find = u.exists() and nxt.exists()
                order = [("max", 0), ("max", 1), ("low", 0), ("max", 2), ("low", 1), ("max", 3), ("turn", 0),
                         ("low", 2), ("low", 3)]
                at = {0: [0, 3, 5, 6, 7], GROUPS - 1: [5, 7]}.get(u.g, [6])
                for n, (what, k) in enumerate(order):
                    for d, place in zip(drains, at):
                        if place == n:
                            d()
                    if find and what == "max":
                        max_piece(nxt, k)
                    if find and what == "turn":
                        max_turned(nxt)
                    if find and what == "low":
                        q_low(nxt, [k])
                if u.exists() and u.g == GROUPS - 1:
                    invert_sums(u)

            for item in range(K_ITEMS):
                br, g = divmod(item, GROUPS)
                dve.wait_ge(k_hi_done, item + 1)
                for j in range(GROUP):
                    rows = slice(j * D, (j + 1) * D)
                    done = nc.vector.scalar_tensor_tensor(
                        out=k_stack[2 * D:3 * D, br, g * GROUP + j],
                        in0=a_ps[item % 2][rows, 0:BATCHES * KEYS].rearrange("p (b n) -> p b n", b=BATCHES),
                        scalar=SCALE, in1=k_diag[rows, br, g, :, j, :].bitcast(F32), op0=ALU.mult, op1=ALU.subtract)
                done.then_inc(k_lo_done, 1)
                for j in range(GROUP):
                    nc.vector.tensor_copy(k_stack[D:2 * D, br, g * GROUP + j],
                                          k_diag[j * D:(j + 1) * D, br, g, :, j, :].bitcast(F32)).then_inc(k_copied, 1)
                if item == 0:
                    q_low(Unit(0, 0), range(GROUP))
            for k in range(MAXES):
                max_piece(Unit(0, 0), k)
            max_turned(Unit(0, 0))
            dve.wait_ge(v_zeroed, 1)
            for item in range(1, V_ITEMS, 2):
                br, b, half = item // 4, item // 2 % 2, item % 2
                dve.wait_ge(v_acc, item + 1)
                nc.vector.tensor_copy(v[0:KEYS, br, b, half * V_COLS:(half + 1) * V_COLS],
                                      b_ps[half][0:KEYS, 0:V_COLS]).then_inc(v_done[half], 1)
            nc.vector.memset(probs[64:P], 0.0).then_inc(probs_zeroed, 1)
            dve.wait_ge(wo_hi_done, 1)
            nc.vector.tensor_tensor(wo_lo[:], stage[1][:, 0:GROUPS * C].rearrange("p (k c) -> p k c", k=GROUPS),
                                    wo_hi[:].bitcast(F32), ALU.subtract).then_inc(wo_lo_done, 1)
            dve.wait_ge(bo_loaded, DMA)
            emit.engine = dve
            stages(emit)

        @block.tensor
        def _(pe):
            def three_pass(out, hi, lo, moving_hi, moving_lo):
                steps = [(w, m, k) for w, m in ((hi, moving_hi), (lo, moving_hi), (hi, moving_lo)) for k in range(GROUPS)]
                for n, (w, m, k) in enumerate(steps):
                    yield lambda w=w, m=m, k=k, n=n: nc.tensor.matmul(
                        out, w(k), m(k), start=(n == 0), stop=(n == len(steps) - 1), skip_group_check=True)

            def project_q(u):
                if u.g == 0:
                    wait(pe, x_hi_done, u.tile(1, 1))
                    wait(pe, x_lo_done, u.tile(1, 1))
                wait(pe, q_low_done, u.number())
                cols = slice(u.g * P, (u.g + 1) * P)
                for step in three_pass(q_ps[:, 0:N], lambda k: wq_hi[:, k, cols], lambda k: wq_lo[:, k, cols],
                                       lambda k: x_hi[:, u.batch, k, :], lambda k: x_lo[:, u.batch, k, :]):
                    done = step()
                done.then_inc(q_acc, 1)

            def max_scores(u, k):
                sub, br = divmod(k, BRANCHES)
                if k == 0:
                    wait(pe, q_hi_done, u.number(1, 1))
                wait(pe, a_drained, u.number(A_ITEMS, k - 1))
                nc.tensor.matmul(a_ps[(u.c * A_ITEMS + k) % 2][:, 0:BLK], q_hi[:, u.slot, sub * P:(sub + 1) * P],
                                 k_diag[:, br, u.g, u.batch].rearrange("p j n -> p (j n)"),
                                 start=True, stop=True).then_inc(a_ready, 1)

            def turn_maxima(u):
                wait(pe, a_drained, u.number(A_ITEMS, MAXES))
                for sub in range(SUB):
                    done = nc.tensor.transpose(
                        a_ps[(u.c * A_ITEMS + MAXES) % 2][0:BRANCHES * GROUP, sub * P:(sub + 1) * P],
                        row_max[:, u.slot, sub, :], ident[:])
                done.then_inc(a_ready, 1)

            def scores(u, j):
                if j == 0:
                    wait(pe, q_top_done, u.number(1, 1))
                    wait(pe, q_low_done, u.number(1, 1))
                    wait(pe, max_in[u.slot], u.uses_of_slot(BRANCHES * DMA))
                wait(pe, b_drained, u.number(GROUP, j - 1))
                for br in range(BRANCHES):
                    done = nc.tensor.matmul(b_ps[j % 2][0:KEYS, br * N:(br + 1) * N],
                                            k_stack[0:STACK, br, u.g * GROUP + j, u.batch, :],
                                            q_stack[0:STACK, u.slot, j, :], start=True, stop=True)
                done.then_inc(b_ready, 1)

            def sums_and_pv(u):
                wait(pe, b_drained, u.number(GROUP, GROUP))
                if u.g == 0:
                    wait(pe, inv_done, u.tile(INV_STEPS))
                wait(pe, pv_drained, u.number())
                for br in range(BRANCHES):
                    c = BRANCHES * u.g + br
                    first = c == 0
                    for j in range(GROUP):
                        nc.tensor.matmul(sum_ps[j * D:(j + 1) * D, 0:N],
                                         sum_first[:] if first else sum_one[:, D - 1 - c:2 * D - 1 - c],
                                         probs[:, j, br * N:(br + 1) * N], start=first,
                                         stop=(c == BRANCHES * GROUPS - 1), skip_group_check=True)
                for br in range(BRANCHES):
                    for j in range(GROUP):
                        h = u.g * GROUP + j
                        done = nc.tensor.matmul(pv_ps[j * D:(j + 1) * D, br * N:(br + 1) * N],
                                                v[:, br, u.batch, h * D:(h + 1) * D],
                                                probs[:, j, br * N:(br + 1) * N], start=True, stop=True)
                done.then_inc(pv_ready, 1)

            def spread_inverse(u):
                if u.g == 0:
                    wait(pe, inv_done, u.tile(INV_STEPS, INV_STEPS))
                wait(pe, x_drained, u.tile(X_ITEMS, u.g))
                for br in range(BRANCHES):
                    sel = spread[:, BRANCHES * u.g + br].rearrange("p j d -> p (j d)")
                    nc.tensor.matmul(x_ps[:, br * N:(br + 1) * N], sel, inv_hi[:], start=True, stop=False,
                                     skip_group_check=True)
                    done = nc.tensor.matmul(x_ps[:, br * N:(br + 1) * N], sel, inv_lo[:], start=False, stop=True,
                                            skip_group_check=True)
                done.then_inc(x_ready, 1)

            def project_out(u, m):
                cols = slice(m * P, (m + 1) * P)
                steps = list(three_pass(x_ps[:, 0:N], lambda k: wo_hi[:, k, cols], lambda k: wo_lo[:, k, cols],
                                        lambda k: attn_hi[:, k, :], lambda k: attn_lo[:, k, :]))

                def first():
                    if m == 0:
                        wait(pe, attn_hi_done, u.number(1, GROUPS))
                        wait(pe, attn_lo_done, u.number(1, GROUPS))
                    wait(pe, x_drained, u.tile(X_ITEMS, GROUPS + m))
                    steps[0]()
                return [first, *steps[1:-1], lambda: steps[-1]().then_inc(x_ready, 1)]

            def emit(u):
                before, nxt = u.tile_plus(-1), u.plus(1)
                find = u.exists() and nxt.exists()
                deal = [[] for _ in range(5)]
                if before.exists():
                    if u.g == 0:
                        deal = [[lambda g=g: spread_inverse(before.plus(g))] for g in range(GROUPS)]
                    elif u.g < GROUPS - 1:
                        s = project_out(before, u.g - 1)
                        deal = [s[0:5], s[5:10], s[10:13], s[13:15], []]
                    else:
                        s = project_out(before, GROUPS - 2)
                        r = project_out(before, GROUPS - 1)
                        deal = [s[0:7], s[7:15], r[0:5], r[5:10], r[10:15]]

                def tile_end(n):
                    for step in deal[n]:
                        step()

                if u.exists():
                    scores(u, 0)
                    scores(u, 1)
                tile_end(0)
                if find:
                    max_scores(nxt, 0)
                    max_scores(nxt, 1)
                if u.exists():
                    scores(u, 2)
                tile_end(1)
                if find:
                    max_scores(nxt, 2)
                if u.exists():
                    scores(u, 3)
                tile_end(2)
                if find:
                    max_scores(nxt, 3)
                tile_end(3)
                if find:
                    turn_maxima(nxt)
                tile_end(4)
                if u.exists():
                    sums_and_pv(u)
                if u.exists() and u.plus(2).exists():
                    project_q(u.plus(2))

            def project_k(item):
                br, g = divmod(item, GROUPS)
                if item % GROUPS == 0:
                    pe.wait_ge(wk_loaded[br], DMA)
                if item >= 2:
                    pe.wait_ge(k_lo_done, item - 1)
                wk = stage[(br + 1) % 2][:].rearrange("p (k c) -> p k c", k=CTX_CHUNKS)
                for k in range(CTX_CHUNKS):
                    done = nc.tensor.matmul(a_ps[item % 2][:, 0:BATCHES * KEYS], wk[:, k, g * P:(g + 1) * P],
                                            ctx[:, k, br].rearrange("p b n -> p (b n)"),
                                            start=(k == 0), stop=(k == CTX_CHUNKS - 1))
                done.then_inc(k_acc, 1)

            def project_v(item):
                br, b, half = item // 4, item // 2 % 2, item % 2
                if item % 4 == 0:
                    pe.wait_ge(wv_loaded[br], DMA)
                if item >= 2:
                    pe.wait_ge(v_done[half], item // 2)
                wv = stage[(br + 1) % 2][:].rearrange("p (k c) -> p k c", k=CTX_CHUNKS)
                for k in range(CTX_CHUNKS):
                    done = nc.tensor.matmul(b_ps[half][0:KEYS, 0:V_COLS], ctx[:, k, br, b, :],
                                            wv[:, k, half * V_COLS:(half + 1) * V_COLS],
                                            start=(k == 0), stop=(k == CTX_CHUNKS - 1))
                done.then_inc(v_acc, 1)

            pe.wait_ge(wq_hi_done, 1)
            pe.wait_ge(wq_lo_done, 1)
            project_q(Unit(0, 0))
            pe.wait_ge(ctx_loaded, DMA)
            for item in range(K_ITEMS):
                project_k(item)
            pe.wait_ge(k_hi_done, K_ITEMS)
            pe.wait_ge(k_lo_done, K_ITEMS)
            project_q(Unit(0, 1))
            for k in range(MAXES):
                max_scores(Unit(0, 0), k)
            pe.wait_ge(consts, 8)
            turn_maxima(Unit(0, 0))
            for item in range(V_ITEMS):
                project_v(item)
            for half in range(2):
                pe.wait_ge(v_done[half], V_ITEMS // 2)
            pe.wait_ge(k_copied, K_ITEMS * BRANCHES * GROUP)
            pe.wait_ge(shift_done, 1 + BRANCHES)
            emit.engine = pe
            stages(emit)


def kernel(x, ctx_2048, L0_xattn_Wq, L0_xattn_Wk, L0_xattn_Wv, L0_xattn_Wk_ip, L0_xattn_Wv_ip, L0_xattn_Wo, L0_xattn_bo):
    import concourse.bacc as bacc
    from concourse.bass_utils import run_bass_kernel_spmd

    def chunked(w):
        w = np.asarray(w)
        return np.ascontiguousarray(w.T.reshape(w.shape[1] // P, P, w.shape[0]).transpose(1, 0, 2)).reshape(P, -1)

    x = np.asarray(x)
    ctx = np.asarray(ctx_2048)
    arrays = {
        "x_in": np.ascontiguousarray(x.reshape(BATCHES, STEPS, N, GROUPS, P).transpose(1, 0, 4, 3, 2)),
        "ctx_in": np.ascontiguousarray(ctx.reshape(BATCHES, BRANCHES, KEYS, CTX_CHUNKS, P).transpose(4, 3, 1, 0, 2)),
        "wq_in": chunked(L0_xattn_Wq),
        "wk_in": np.stack([chunked(L0_xattn_Wk), chunked(L0_xattn_Wk_ip)]),
        "wv_in": np.stack([chunked(L0_xattn_Wv), chunked(L0_xattn_Wv_ip)]),
        "wo_in": chunked(L0_xattn_Wo),
        "bo_in": np.ascontiguousarray(np.asarray(L0_xattn_bo).reshape(GROUPS, P).T),
    }
    nc = bacc.Bacc("TRN2", target_bir_lowering=False, num_devices=1)
    args = [nc.dram_tensor(name, a.shape, mybir.dt.from_np(a.dtype), kind="ExternalInput").ap()
            for name, a in arrays.items()]
    out = nc.dram_tensor("y_out", (STEPS, BATCHES, P, GROUPS, N), F32, kind="ExternalOutput").ap()
    build(nc, *args, out)
    y = run_bass_kernel_spmd(nc, [arrays], core_ids=[0]).results[0]["y_out"]
    return np.ascontiguousarray(y.transpose(1, 0, 4, 3, 2)).reshape(BATCHES, SEQ, C)
```

```python
from contextlib import ExitStack

import numpy as np

import concourse.bass as bass
from concourse import mybir

ACT = mybir.ActivationFunctionType
ALU = mybir.AluOpType
AXIS = mybir.AxisListType
F32 = mybir.dt.float32
F32R = mybir.dt.float32r

P = 128
BATCHES, SEQ, C, CTX_C = 2, 2048, 640, 1024
HEADS, KEYS, BRANCHES = 20, 77, 2
D = C // HEADS
SCALE = float(np.float32(1.0) / np.sqrt(np.float32(D)))
GROUP = P // D
GROUPS = C // P
CTX_CHUNKS = CTX_C // P
N = 256
SUB = N // P
TILES = BATCHES * SEQ // N
STEPS = TILES // BATCHES
UNITS = TILES * GROUPS
BLK = GROUP * KEYS
SHIFT_ROW = 3 * D
STACK = SHIFT_ROW + BRANCHES
MAXES = SUB * BRANCHES
A_ITEMS = MAXES + 1
X_ITEMS = 2 * GROUPS
V_COLS = C // 2
DMA = 16


class Unit:

    def __init__(self, t, c):
        carry, c = divmod(c, GROUPS * BATCHES)
        self.t, self.c = t + carry, c
        self.batch, self.g = divmod(c, GROUPS)
        self.slot = c % 2
        self.fixed = isinstance(self.t, int)

    def plus(self, k):
        return Unit(self.t, self.c + k)

    def tile_plus(self, k):
        return Unit(self.t, self.c - self.g + k * GROUPS)

    def number(self, scale=1, plus=0):
        return self.t * (GROUPS * BATCHES * scale) + (self.c * scale + plus)

    def tile(self, scale=1, plus=0):
        return self.t * (BATCHES * scale) + (self.batch * scale + plus)

    def uses_of_slot(self, scale=1):
        return self.t * (GROUPS * BATCHES // 2 * scale) + (self.c // 2 + 1) * scale

    def exists(self):
        return not self.fixed or 0 <= self.t < STEPS


def wait(eng, sem, value):
    if not isinstance(value, int) or value > 0:
        eng.wait_ge(sem, value)


def build(nc, x_d, ctx_d, wq_d, wk_d, wv_d, wo_d, bo_d, out_d):
    with ExitStack() as stack:
        def sbuf(name, shape, dt=F32, scope=stack):
            return scope.enter_context(nc.sbuf_tensor(name, shape, dt))

        def psum(name):
            return stack.enter_context(nc.psum_tensor(name, [P, 512], F32))

        def sem(name):
            return stack.enter_context(nc.semaphore(name))

        wq_hi = sbuf("wq_hi", [P, GROUPS, C], F32R)
        wq_lo = sbuf("wq_lo", [P, GROUPS, C], F32R)
        wo_hi = sbuf("wo_hi", [P, GROUPS, C], F32R)
        wo_lo = sbuf("wo_lo", [P, GROUPS, C], F32R)
        k_stack = sbuf("k_stack", [P, BRANCHES, HEADS, BATCHES, KEYS], F32R)
        k_diag = sbuf("k_diag", [P, BRANCHES, GROUPS, BATCHES, GROUP, KEYS], F32R)
        v = sbuf("v", [P, BRANCHES, BATCHES, C])
        bo = sbuf("bo", [P, GROUPS])
        ident = sbuf("ident", [P, P])
        sum_first = sbuf("sum_first", [P, D])
        sum_one = sbuf("sum_one", [P, 2 * D])
        spread = sbuf("spread", [P, BRANCHES * GROUPS, GROUP, D], F32R)
        x_raw = sbuf("x_raw", [P, GROUPS, N])
        x_hi = sbuf("x_hi", [P, BATCHES, GROUPS, N], F32R)
        x_lo = sbuf("x_lo", [P, BATCHES, GROUPS, N], F32R)
        q_hi = sbuf("q_hi", [P, 2, N], F32R)
        q_stack = sbuf("q_stack", [P, 2, GROUP, N], F32R)
        row_max = sbuf("row_max", [P, 2, SUB, BRANCHES * GROUP])
        max_rows = sbuf("max_rows", [BRANCHES * GROUP, 2, N], F32R)
        stage = [sbuf(f"stage{i}", [P, CTX_CHUNKS * C]) for i in range(2)]
        probs = stage[0][:, 0:GROUP * BRANCHES * N].rearrange("p (j n) -> p j n", j=GROUP)
        scaled = stage[0][:, GROUP * BRANCHES * N:][:, 0:2 * BRANCHES * N].rearrange("p (s n) -> p s n", s=2)
        pv_sb = stage[1][:, 0:GROUPS * BRANCHES * N].rearrange("p (g n) -> p g n", g=GROUPS)
        attn = stage[1][:, GROUPS * BRANCHES * N:][:, 0:GROUPS * N].rearrange("p (g n) -> p g n", g=GROUPS)
        res = stage[1][:, GROUPS * (BRANCHES + 1) * N:][:, 0:GROUPS * N].rearrange("p (g n) -> p g n", g=GROUPS)
        with ExitStack() as before:
            ctx = sbuf("ctx", [P, CTX_CHUNKS, BRANCHES, BATCHES, KEYS], scope=before)
        attn_hi = sbuf("attn_hi", [P, GROUPS, N], F32R)
        attn_lo = sbuf("attn_lo", [P, GROUPS, N], F32R)
        inv = sbuf("inv", [P, N])
        inv_hi = sbuf("inv_hi", [P, N], F32R)
        inv_lo = sbuf("inv_lo", [P, N], F32R)

        q_ps = psum("q_ps")
        x_ps = psum("x_ps")
        a_ps = [psum("a_ps0"), psum("a_ps1")]
        b_ps = [psum("b_ps0"), psum("b_ps1")]
        pv_ps = psum("pv_ps")
        sum_ps = psum("sum_ps")

        x_loaded = sem("x_loaded")
        wq_loaded = sem("wq_loaded")
        ctx_loaded = sem("ctx_loaded")
        bo_loaded = sem("bo_loaded")
        wk_loaded = [sem(f"wk_loaded{br}") for br in range(BRANCHES)]
        wv_loaded = [sem(f"wv_loaded{br}") for br in range(BRANCHES)]
        wo_loaded = sem("wo_loaded")
        wq_hi_done, wq_lo_done = sem("wq_hi_done"), sem("wq_lo_done")
        wo_hi_done, wo_lo_done = sem("wo_hi_done"), sem("wo_lo_done")
        zeroed = sem("zeroed")
        consts = sem("consts")
        shift_done = sem("shift_done")
        k_acc = sem("k_acc")
        k_hi_done = sem("k_hi_done")
        k_lo_done = sem("k_lo_done")
        k_copied = sem("k_copied")
        v_acc = sem("v_acc")
        v_done = [sem(f"v_done{half}") for half in range(2)]
        v_zeroed = sem("v_zeroed")
        probs_zeroed = sem("probs_zeroed")
        x_hi_done, x_lo_done = sem("x_hi_done"), sem("x_lo_done")
        q_acc = sem("q_acc")
        q_hi_done = sem("q_hi_done")
        q_top_done = sem("q_top_done")
        q_low_done = sem("q_low_done")
        q_third = [sem(f"q_third{s}") for s in range(2)]
        a_ready, a_drained = sem("a_ready"), sem("a_drained")
        max_in = [sem(f"max_in{s}") for s in range(2)]
        b_ready, b_drained = sem("b_ready"), sem("b_drained")
        pv_ready = sem("pv_ready")
        pv_drained = sem("pv_drained")
        inv_done = sem("inv_done")
        x_ready, x_drained = sem("x_ready"), sem("x_drained")
        attn_done = sem("attn_done")
        attn_hi_done, attn_lo_done = sem("attn_hi_done"), sem("attn_lo_done")
        res_loaded = sem("res_loaded")
        stored = sem("stored")

        INV_STEPS = 3
        K_ITEMS = BRANCHES * GROUPS
        V_ITEMS = BRANCHES * BATCHES * (C // V_COLS)
        TAIL = GROUPS + 2
        block = stack.enter_context(nc.Block())

        def stages(emit):
            def pair(t):
                for c in range(GROUPS * BATCHES):
                    emit(Unit(t, c))
            pair(0)
            with emit.engine.Fori(1, STEPS - 1) as t:
                pair(t)
            pair(STEPS - 1)
            for c in range(TAIL):
                emit(Unit(STEPS, c))

        @block.sync
        def _(sp):
            sp.dma_start(x_raw[:], x_d[0, 0]).then_inc(x_loaded, DMA)
            sp.dma_start(stage[0][:, 0:GROUPS * C], wq_d).then_inc(wq_loaded, DMA)
            sp.dma_start(ctx[:], ctx_d).then_inc(ctx_loaded, DMA)
            sp.dma_start(stage[1][:], wk_d[0]).then_inc(wk_loaded[0], DMA)
            sp.dma_start(bo[:], bo_d).then_inc(bo_loaded, DMA)
            sp.wait_ge(wq_lo_done, 1)
            sp.dma_start(stage[0][:], wk_d[1]).then_inc(wk_loaded[1], DMA)
            sp.wait_ge(x_lo_done, 1)
            sp.dma_start(x_raw[:], x_d[0, 1]).then_inc(x_loaded, DMA)
            sp.wait_ge(k_acc, GROUPS)
            sp.dma_start(stage[1][:], wv_d[0]).then_inc(wv_loaded[0], DMA)
            sp.wait_ge(k_acc, K_ITEMS)
            sp.dma_start(stage[0][:], wv_d[1]).then_inc(wv_loaded[1], DMA)
            sp.wait_ge(v_acc, V_ITEMS // 2)
            sp.dma_start(stage[1][:, 0:GROUPS * C], wo_d).then_inc(wo_loaded, DMA)

            def maxima(u):
                wait(sp, a_drained, u.number(A_ITEMS, A_ITEMS))
                for br in range(BRANCHES):
                    sp.dma_start(q_stack[SHIFT_ROW + br:SHIFT_ROW + br + 1, u.slot].bitcast(F32),
                                 max_rows[br * GROUP:(br + 1) * GROUP, u.slot, :].bitcast(F32)).then_inc(max_in[u.slot], DMA)

            def store(u, m):
                wait(sp, x_drained, u.tile(X_ITEMS, GROUPS + m + 1))
                sp.dma_start(out_d[u.t, u.batch, :, m, :], res[:, m, :]).then_inc(stored, DMA)

            def third_block(u):
                wait(sp, q_top_done, u.number(1, 1))
                sp.dma_start(q_stack[2 * D:3 * D, u.slot].bitcast(F32),
                             q_stack[0:D, u.slot].bitcast(F32)).then_inc(q_third[u.slot], DMA)

            def emit(u):
                before, ahead = u.tile_plus(-1), u.tile_plus(2)
                for back, m in {0: [(-1, 3)], 1: [(-2, 4)], 3: [(-1, 0), (-1, 1)], 4: [(-1, 2)]}.get(u.g, []):
                    tile = u.tile_plus(back - (u.g == 0))
                    if tile.exists():
                        store(tile, m)
                if u.exists() and u.plus(1).exists():
                    maxima(u.plus(1))
                if u.exists() and u.plus(2).exists():
                    third_block(u.plus(2))
                if u.g == 1 and before.exists():
                    wait(sp, stored, before.tile(GROUPS * DMA))
                    if before.fixed and before.number() == 0:
                        sp.wait_ge(wo_lo_done, 1)
                    sp.dma_start(res[:], x_d[before.t, before.batch]).then_inc(res_loaded, DMA)
                if u.g == 1 and u.exists() and ahead.exists():
                    wait(sp, x_lo_done, u.tile(1, 2))
                    sp.dma_start(x_raw[:], x_d[ahead.t, ahead.batch]).then_inc(x_loaded, DMA)

            third_block(Unit(0, 0))
            maxima(Unit(0, 0))
            third_block(Unit(0, 1))
            emit.engine = sp
            stages(emit)
            sp.wait_ge(stored, TILES * GROUPS * DMA)

        @block.gpsimd
        def _(pool):
            nc.gpsimd.memset(ident[:], 0.0).then_inc(consts, 1)
            pool.wait_ge(consts, 1)
            nc.gpsimd.affine_select(out=ident[:], in_=ident[:], compare_op=ALU.not_equal, fill=1.0, base=0,
                                    pattern=[[-1, P]], channel_multiplier=1).then_inc(consts, 1)
            nc.gpsimd.memset(sum_one[:], 0.0).then_inc(consts, 1)
            nc.gpsimd.memset(sum_first[:], 1.0).then_inc(consts, 1)
            pool.wait_ge(consts, 4)
            nc.gpsimd.memset(sum_one[:, D - 1:D], 1.0).then_inc(consts, 1)
            nc.gpsimd.memset(sum_first[:, 1:BRANCHES * GROUPS], 0.0).then_inc(consts, 1)
            nc.gpsimd.memset(k_diag[:, 1].bitcast(F32), 0.0).then_inc(zeroed, 1)
            nc.gpsimd.memset(spread[:].bitcast(F32), 0.0).then_inc(consts, 1)
            pool.wait_ge(consts, 7)
            nc.gpsimd.affine_select(out=spread[:], in_=spread[:], compare_op=ALU.not_equal, fill=1.0, base=0,
                                    pattern=[[-1, BRANCHES * GROUPS], [-D, GROUP], [0, D]],
                                    channel_multiplier=1).then_inc(consts, 1)

            def split_x(u):
                wait(pool, x_hi_done, u.tile(1, 1))
                nc.gpsimd.tensor_tensor(x_lo[:, u.batch], x_raw[:], x_hi[:, u.batch].bitcast(F32),
                                        ALU.subtract).then_inc(x_lo_done, 1)

            def add_branches(u):
                n = u.tile(X_ITEMS, u.g + 1)
                wait(pool, x_drained, n)
                s = u.slot
                nc.gpsimd.tensor_tensor(attn[:, u.g, :], scaled[:, s, 0:N], scaled[:, s, N:2 * N],
                                        ALU.add).then_inc(attn_done, 1)

            def attn_low(u):
                wait(pool, attn_hi_done, u.number(1, 1))
                nc.gpsimd.tensor_tensor(attn_lo[:, u.g, :], attn[:, u.g, :], attn_hi[:, u.g, :].bitcast(F32),
                                        ALU.subtract).then_inc(attn_lo_done, 1)

            def emit(u):
                before, ahead = u.tile_plus(-1), u.tile_plus(1)
                if u.g == 0 and u.exists() and ahead.exists() and not (u.fixed and u.number() == 0):
                    split_x(ahead)
                if before.exists():
                    for step, g in {1: [(add_branches, 0), (attn_low, 0), (add_branches, 1), (attn_low, 1)],
                                    2: [(add_branches, 2), (add_branches, 3), (attn_low, 2), (add_branches, 4),
                                        (attn_low, 3), (attn_low, 4)]}.get(u.g, []):
                        step(before.plus(g))

            split_x(Unit(0, 0))
            split_x(Unit(0, GROUPS))
            emit.engine = pool
            stages(emit)

        @block.scalar
        def _(act):
            act.wait_ge(x_loaded, DMA)
            nc.scalar.activation(x_hi[:, 0], x_raw[:], ACT.Copy).then_inc(x_hi_done, 1)
            act.wait_ge(wq_loaded, DMA)
            nc.scalar.activation(wq_hi[:], stage[0][:, 0:GROUPS * C].rearrange("p (k c) -> p k c", k=GROUPS),
                                 ACT.Copy).then_inc(wq_hi_done, 1)

            def q_high(u):
                wait(act, q_acc, u.number(1, 1))
                wait(act, a_ready, u.number(A_ITEMS, -A_ITEMS))
                wait(act, q_low_done, u.number(1, -1))
                nc.scalar.activation(q_hi[:, u.slot, :], q_ps[:, 0:N], ACT.Copy).then_inc(q_hi_done, 1)

            def q_top(u, heads):
                wait(act, b_ready, u.number(GROUP, -GROUP))
                wait(act, q_hi_done, u.number(1, 1))
                for j in heads:
                    done = nc.scalar.activation(q_stack[0:D, u.slot, j, :],
                                                q_hi[j * D:(j + 1) * D, u.slot, :].bitcast(F32), ACT.Copy)
                    if j == GROUP - 1:
                        done.then_inc(q_top_done, 1)

            def exp(u, j):
                wait(act, b_ready, u.number(GROUP, j + 1))
                if j == 0:
                    wait(act, pv_ready, u.number())
                nc.scalar.activation(probs[0:KEYS, j, :], b_ps[j % 2][0:KEYS, :], ACT.Exp).then_inc(b_drained, 1)

            def keep_pv(u):
                wait(act, pv_ready, u.number(1, 1))
                wait(act, x_drained, u.tile(X_ITEMS, u.g + 1 - X_ITEMS))
                nc.scalar.activation(pv_sb[:, u.g, :], pv_ps[:], ACT.Copy).then_inc(pv_drained, 1)

            def split_x(u):
                wait(act, x_loaded, u.tile(DMA, DMA))
                wait(act, q_acc, u.number(1, -GROUPS))
                nc.scalar.activation(x_hi[:, u.batch], x_raw[:], ACT.Copy).then_inc(x_hi_done, 1)

            def attn_high(u):
                wait(act, attn_done, u.number(1, 1))
                nc.scalar.activation(attn_hi[:, u.g, :], attn[:, u.g, :], ACT.Copy).then_inc(attn_hi_done, 1)

            def emit(u):
                before, ahead, nxt = u.tile_plus(-1), u.tile_plus(2), u.plus(2)

                def attn_parts(*groups):
                    if before.exists():
                        for g in groups:
                            attn_high(before.plus(g))

                if u.exists():
                    exp(u, 0)
                    exp(u, 1)
                if u.plus(-1).exists():
                    keep_pv(u.plus(-1))
                if u.g == 2:
                    attn_parts(2)
                if u.exists():
                    exp(u, 2)
                    exp(u, 3)
                if u.g == 2:
                    attn_parts(3, 4)
                if u.exists() and nxt.exists():
                    q_high(nxt)
                    q_top(nxt, range(GROUP))
                if u.g == 1:
                    attn_parts(0, 1)
                if u.g == GROUPS - 1 and u.exists() and ahead.exists():
                    split_x(ahead)

            act.wait_ge(zeroed, 2)
            for item in range(K_ITEMS):
                br, g = divmod(item, GROUPS)
                act.wait_ge(k_acc, item + 1)
                for j in range(GROUP):
                    rows = slice(j * D, (j + 1) * D)
                    done = nc.scalar.activation(
                        k_diag[rows, br, g, :, j, :],
                        a_ps[item % 2][rows, 0:BATCHES * KEYS].rearrange("p (b n) -> p b n", b=BATCHES),
                        ACT.Copy, scale=SCALE)
                done.then_inc(k_hi_done, 1)
                act.wait_ge(k_hi_done, item + 1)
                for j in range(GROUP):
                    nc.scalar.activation(k_stack[0:D, br, g * GROUP + j], k_diag[j * D:(j + 1) * D, br, g, :, j, :].bitcast(F32),
                                         ACT.Copy).then_inc(k_copied, 1)
                if item == 0:
                    q_high(Unit(0, 0))
                    q_top(Unit(0, 0), range(GROUP))
            q_high(Unit(0, 1))
            q_top(Unit(0, 1), range(GROUP))
            split_x(Unit(0, GROUPS))
            act.wait_ge(v_zeroed, 1)
            for item in range(0, V_ITEMS, 2):
                br, b, half = item // 4, item // 2 % 2, item % 2
                act.wait_ge(v_acc, item + 1)
                nc.scalar.activation(v[0:KEYS, br, b, half * V_COLS:(half + 1) * V_COLS],
                                     b_ps[half][0:KEYS, 0:V_COLS], ACT.Copy).then_inc(v_done[half], 1)
            act.wait_ge(wo_loaded, DMA)
            nc.scalar.activation(wo_hi[:], stage[1][:, 0:GROUPS * C].rearrange("p (k c) -> p k c", k=GROUPS),
                                 ACT.Copy).then_inc(wo_hi_done, 1)
            act.wait_ge(probs_zeroed, 1)
            act.wait_ge(wo_lo_done, 1)
            emit.engine = act
            stages(emit)

        @block.vector
        def _(dve):
            nc.vector.memset(k_diag[:, 0].bitcast(F32), 0.0).then_inc(zeroed, 1)
            nc.vector.memset(k_stack[SHIFT_ROW:STACK].bitcast(F32), 1.0).then_inc(shift_done, 1)
            nc.vector.memset(v[64:P], 0.0).then_inc(v_zeroed, 1)
            dve.wait_ge(wq_hi_done, 1)
            nc.vector.tensor_tensor(wq_lo[:], stage[0][:, 0:GROUPS * C].rearrange("p (k c) -> p k c", k=GROUPS),
                                    wq_hi[:].bitcast(F32), ALU.subtract).then_inc(wq_lo_done, 1)
            dve.wait_ge(consts, 2)
            dve.wait_ge(shift_done, 1)
            for br in range(BRANCHES):
                pick = ident[SHIFT_ROW:STACK, SHIFT_ROW + br:SHIFT_ROW + br + 1]
                nc.vector.tensor_scalar(k_stack[SHIFT_ROW:STACK, br], k_stack[SHIFT_ROW:STACK, br].bitcast(F32),
                                        pick, -1.0, ALU.mult, ALU.mult).then_inc(shift_done, 1)

            def q_low(u):
                wait(dve, q_hi_done, u.number(1, 1))
                wait(dve, b_ready, u.number(GROUP, -GROUP))
                for j in range(GROUP):
                    rows = slice(j * D, (j + 1) * D)
                    done = nc.vector.tensor_tensor(q_stack[D:2 * D, u.slot, j, :], q_ps[rows, 0:N],
                                                   q_hi[rows, u.slot, :].bitcast(F32), ALU.subtract)
                done.then_inc(q_low_done, 1)

            def max_piece(u, k):
                item = u.number(A_ITEMS, k)
                sub, br = divmod(k, BRANCHES)
                wait(dve, a_ready, u.number(A_ITEMS, k + 1))
                bank = a_ps[(u.c * A_ITEMS + k) % 2]
                nc.vector.tensor_reduce(row_max[:, u.slot, sub, br * GROUP:(br + 1) * GROUP],
                                        bank[:, 0:BLK].rearrange("p (j n) -> p j n", j=GROUP), AXIS.X,
                                        ALU.max).then_inc(a_drained, 1)

            def max_turned(u):
                wait(dve, a_ready, u.number(A_ITEMS, A_ITEMS))
                wait(dve, max_in[u.slot], u.uses_of_slot(BRANCHES * DMA) - BRANCHES * DMA)
                nc.vector.tensor_copy(max_rows[:, u.slot, :],
                                      a_ps[(u.c * A_ITEMS + MAXES) % 2][0:BRANCHES * GROUP, 0:N]).then_inc(a_drained, 1)

            def invert_sums(u):
                wait(dve, pv_ready, u.number(1, GROUPS))
                wait(dve, x_ready, u.tile(X_ITEMS, GROUPS - X_ITEMS))
                nc.vector.reciprocal(inv[:], sum_ps[:, 0:N]).then_inc(inv_done, 1)
                wait(dve, inv_done, u.tile(INV_STEPS, 1))
                nc.vector.tensor_copy(inv_hi[:], inv[:]).then_inc(inv_done, 1)
                wait(dve, inv_done, u.tile(INV_STEPS, 2))
                nc.vector.tensor_tensor(inv_lo[:], inv[:], inv_hi[:].bitcast(F32), ALU.subtract).then_inc(inv_done, 1)

            def normalise(u):
                wait(dve, x_ready, u.tile(X_ITEMS, u.g + 1))
                wait(dve, pv_drained, u.number(1, 1))
                wait(dve, attn_done, u.number(1, -1))
                nc.vector.tensor_tensor(scaled[:, u.slot, :], x_ps[:], pv_sb[:, u.g, :],
                                        ALU.mult).then_inc(x_drained, 1)

            def finish(u, m):
                wait(dve, x_ready, u.tile(X_ITEMS, GROUPS + m + 1))
                if m == 0:
                    wait(dve, res_loaded, u.tile(DMA, DMA))
                nc.vector.scalar_tensor_tensor(out=res[:, m, :], in0=x_ps[:, 0:N], scalar=bo[:, m:m + 1],
                                               in1=res[:, m, :], op0=ALU.add, op1=ALU.add).then_inc(x_drained, 1)

            def emit(u):
                before, nxt = u.tile_plus(-1), u.plus(1)

                def turn(k):
                    if u.exists() and nxt.exists():
                        max_piece(nxt, k) if k < MAXES else max_turned(nxt)

                def end(what, k):
                    if before.exists():
                        what(before.plus(k)) if what is normalise else what(before, k)

                turn(0)
                turn(1)
                if u.g == 1:
                    end(normalise, 1)
                if u.g == 2:
                    end(normalise, 4)
                turn(2)
                turn(3)
                turn(MAXES)
                if u.g == 0 and before.exists():
                    invert_sums(before)
                if u.g == 0 and u.tile_plus(-2).exists():
                    finish(u.tile_plus(-2), 4)
                if u.g == 1:
                    end(normalise, 2)
                if u.exists() and u.plus(2).exists():
                    q_low(u.plus(2))
                if u.g == 0:
                    end(normalise, 0)
                if u.g == 1:
                    end(normalise, 3)
                for m in {2: (0, 1), 3: (2,), 4: (3,)}.get(u.g, ()):
                    end(finish, m)

            for item in range(K_ITEMS):
                br, g = divmod(item, GROUPS)
                dve.wait_ge(k_hi_done, item + 1)
                for j in range(GROUP):
                    rows = slice(j * D, (j + 1) * D)
                    done = nc.vector.scalar_tensor_tensor(
                        out=k_stack[2 * D:3 * D, br, g * GROUP + j],
                        in0=a_ps[item % 2][rows, 0:BATCHES * KEYS].rearrange("p (b n) -> p b n", b=BATCHES),
                        scalar=SCALE, in1=k_diag[rows, br, g, :, j, :].bitcast(F32), op0=ALU.mult, op1=ALU.subtract)
                done.then_inc(k_lo_done, 1)
                for j in range(GROUP):
                    nc.vector.tensor_copy(k_stack[D:2 * D, br, g * GROUP + j],
                                          k_diag[j * D:(j + 1) * D, br, g, :, j, :].bitcast(F32)).then_inc(k_copied, 1)
                if item == 0:
                    q_low(Unit(0, 0))
            for k in range(MAXES):
                max_piece(Unit(0, 0), k)
            max_turned(Unit(0, 0))
            q_low(Unit(0, 1))
            dve.wait_ge(v_zeroed, 1)
            for item in range(1, V_ITEMS, 2):
                br, b, half = item // 4, item // 2 % 2, item % 2
                dve.wait_ge(v_acc, item + 1)
                nc.vector.tensor_copy(v[0:KEYS, br, b, half * V_COLS:(half + 1) * V_COLS],
                                      b_ps[half][0:KEYS, 0:V_COLS]).then_inc(v_done[half], 1)
            nc.vector.memset(probs[64:P], 0.0).then_inc(probs_zeroed, 1)
            dve.wait_ge(wo_hi_done, 1)
            nc.vector.tensor_tensor(wo_lo[:], stage[1][:, 0:GROUPS * C].rearrange("p (k c) -> p k c", k=GROUPS),
                                    wo_hi[:].bitcast(F32), ALU.subtract).then_inc(wo_lo_done, 1)
            dve.wait_ge(bo_loaded, DMA)
            emit.engine = dve
            stages(emit)

        @block.tensor
        def _(pe):
            def three_pass(out, hi, lo, moving_hi, moving_lo):
                steps = [(w, m, k) for w, m in ((hi, moving_hi), (lo, moving_hi), (hi, moving_lo)) for k in range(GROUPS)]
                for n, (w, m, k) in enumerate(steps):
                    yield lambda w=w, m=m, k=k, n=n: nc.tensor.matmul(
                        out, w(k), m(k), start=(n == 0), stop=(n == len(steps) - 1), skip_group_check=True)

            def project_q(u):
                cols = slice(u.g * P, (u.g + 1) * P)
                steps = list(three_pass(q_ps[:, 0:N], lambda k: wq_hi[:, k, cols], lambda k: wq_lo[:, k, cols],
                                        lambda k: x_hi[:, u.batch, k, :], lambda k: x_lo[:, u.batch, k, :]))


                def first():
                    if u.g == 0:
                        wait(pe, x_lo_done, u.tile(1, 1))
                    wait(pe, q_low_done, u.number())
                    steps[0]()
                return [first, *steps[1:-1], lambda: steps[-1]().then_inc(q_acc, 1)]

            def max_scores(u, k):
                sub, br = divmod(k, BRANCHES)
                if k == 0:
                    wait(pe, q_hi_done, u.number(1, 1))
                wait(pe, a_drained, u.number(A_ITEMS, k - 1))
                nc.tensor.matmul(a_ps[(u.c * A_ITEMS + k) % 2][:, 0:BLK], q_hi[:, u.slot, sub * P:(sub + 1) * P],
                                 k_diag[:, br, u.g, u.batch].rearrange("p j n -> p (j n)"),
                                 start=True, stop=True).then_inc(a_ready, 1)

            def turn_maxima(u):
                wait(pe, a_drained, u.number(A_ITEMS, MAXES))
                for sub in range(SUB):
                    done = nc.tensor.transpose(
                        a_ps[(u.c * A_ITEMS + MAXES) % 2][0:BRANCHES * GROUP, sub * P:(sub + 1) * P],
                        row_max[:, u.slot, sub, :], ident[:])
                done.then_inc(a_ready, 1)

            def scores(u, j):
                if j == 0:
                    wait(pe, q_low_done, u.number(1, 1))
                    wait(pe, q_third[u.slot], u.uses_of_slot(DMA))
                    wait(pe, max_in[u.slot], u.uses_of_slot(BRANCHES * DMA))
                wait(pe, b_drained, u.number(GROUP, j - 1))
                for br in range(BRANCHES):
                    done = nc.tensor.matmul(b_ps[j % 2][0:KEYS, br * N:(br + 1) * N],
                                            k_stack[0:STACK, br, u.g * GROUP + j, u.batch, :],
                                            q_stack[0:STACK, u.slot, j, :], start=True, stop=True)
                done.then_inc(b_ready, 1)

            def sums_and_pv(u):
                wait(pe, b_drained, u.number(GROUP, GROUP))
                if u.g == 0:
                    wait(pe, inv_done, u.tile(INV_STEPS, 1 - INV_STEPS))
                wait(pe, pv_drained, u.number())
                for br in range(BRANCHES):
                    c = BRANCHES * u.g + br
                    first = c == 0
                    for j in range(GROUP):
                        nc.tensor.matmul(sum_ps[j * D:(j + 1) * D, 0:N],
                                         sum_first[:] if first else sum_one[:, D - 1 - c:2 * D - 1 - c],
                                         probs[:, j, br * N:(br + 1) * N], start=first,
                                         stop=(c == BRANCHES * GROUPS - 1), skip_group_check=True)
                for br in range(BRANCHES):
                    for j in range(GROUP):
                        h = u.g * GROUP + j
                        done = nc.tensor.matmul(pv_ps[j * D:(j + 1) * D, br * N:(br + 1) * N],
                                                v[:, br, u.batch, h * D:(h + 1) * D],
                                                probs[:, j, br * N:(br + 1) * N], start=True, stop=True)
                done.then_inc(pv_ready, 1)

            def spread_inverse(u):
                if u.g == 0:
                    wait(pe, inv_done, u.tile(INV_STEPS, INV_STEPS))
                wait(pe, x_drained, u.tile(X_ITEMS, u.g))
                for br in range(BRANCHES):
                    sel = spread[:, BRANCHES * u.g + br].rearrange("p j d -> p (j d)")
                    nc.tensor.matmul(x_ps[:, br * N:(br + 1) * N], sel, inv_hi[:], start=True, stop=False,
                                     skip_group_check=True)
                    done = nc.tensor.matmul(x_ps[:, br * N:(br + 1) * N], sel, inv_lo[:], start=False, stop=True,
                                            skip_group_check=True)
                done.then_inc(x_ready, 1)

            def project_out(u, m):
                cols = slice(m * P, (m + 1) * P)
                steps = list(three_pass(x_ps[:, 0:N], lambda k: wo_hi[:, k, cols], lambda k: wo_lo[:, k, cols],
                                        lambda k: attn_hi[:, k, :], lambda k: attn_lo[:, k, :]))

                def first():
                    if m == 0:
                        wait(pe, attn_hi_done, u.number(1, GROUPS))
                    wait(pe, x_drained, u.tile(X_ITEMS, GROUPS + m))
                    steps[0]()

                def first_low():
                    if m == 0:
                        wait(pe, attn_lo_done, u.number(1, GROUPS))
                    steps[2 * GROUPS]()
                return [first, *steps[1:2 * GROUPS], first_low, *steps[2 * GROUPS + 1:-1],
                        lambda: steps[-1]().then_inc(x_ready, 1)]

            def emit(u):
                before, nxt = u.tile_plus(-1), u.plus(1)
                find = u.exists() and nxt.exists()
                q = project_q(u.plus(2)) if u.exists() and u.plus(2).exists() else []
                tile, chunk = (u.tile_plus(-2), 4) if u.g == 0 else (before, {2: 0, 3: 2, 4: 3}.get(u.g))
                out = project_out(tile, chunk) if tile.exists() and chunk is not None else []

                def run(steps):
                    for step in steps:
                        step()

                def spread_to(g):
                    if before.exists():
                        spread_inverse(before.plus(g))

                def find_max(k):
                    if find:
                        max_scores(nxt, k) if k < MAXES else turn_maxima(nxt)

                def score(j):
                    if u.exists():
                        scores(u, j)

                find_max(0)
                find_max(1)
                score(0)
                score(1)
                if u.g == 1:
                    spread_to(1)
                if u.g == 2:
                    spread_to(4)
                run(q[:5])
                find_max(2)
                score(2)
                find_max(3)
                score(3)
                run(q[5:10])
                find_max(MAXES)
                if u.g == 1:
                    spread_to(2)
                run(q[10:])
                run(out)
                if u.exists():
                    sums_and_pv(u)
                if u.g == 0:
                    spread_to(0)
                if u.g == 1:
                    spread_to(3)
                if u.g == 2 and before.exists():
                    run(project_out(before, 1))

            def project_k(item):
                br, g = divmod(item, GROUPS)
                if item % GROUPS == 0:
                    pe.wait_ge(wk_loaded[br], DMA)
                if item >= 2:
                    pe.wait_ge(k_lo_done, item - 1)
                wk = stage[(br + 1) % 2][:].rearrange("p (k c) -> p k c", k=CTX_CHUNKS)
                for k in range(CTX_CHUNKS):
                    done = nc.tensor.matmul(a_ps[item % 2][:, 0:BATCHES * KEYS], wk[:, k, g * P:(g + 1) * P],
                                            ctx[:, k, br].rearrange("p b n -> p (b n)"),
                                            start=(k == 0), stop=(k == CTX_CHUNKS - 1))
                done.then_inc(k_acc, 1)

            def project_v(item):
                br, b, half = item // 4, item // 2 % 2, item % 2
                if item % 4 == 0:
                    pe.wait_ge(wv_loaded[br], DMA)
                if item >= 2:
                    pe.wait_ge(v_done[half], item // 2)
                wv = stage[(br + 1) % 2][:].rearrange("p (k c) -> p k c", k=CTX_CHUNKS)
                for k in range(CTX_CHUNKS):
                    done = nc.tensor.matmul(b_ps[half][0:KEYS, 0:V_COLS], ctx[:, k, br, b, :],
                                            wv[:, k, half * V_COLS:(half + 1) * V_COLS],
                                            start=(k == 0), stop=(k == CTX_CHUNKS - 1))
                done.then_inc(v_acc, 1)

            pe.wait_ge(wq_lo_done, 1)
            for step in project_q(Unit(0, 0)):
                step()
            pe.wait_ge(ctx_loaded, DMA)
            for item in range(K_ITEMS):
                project_k(item)
            pe.wait_ge(k_hi_done, K_ITEMS)
            pe.wait_ge(k_lo_done, K_ITEMS)
            for step in project_q(Unit(0, 1)):
                step()
            for k in range(MAXES):
                max_scores(Unit(0, 0), k)
            pe.wait_ge(consts, 8)
            turn_maxima(Unit(0, 0))
            for item in range(V_ITEMS):
                project_v(item)
            for half in range(2):
                pe.wait_ge(v_done[half], V_ITEMS // 2)
            pe.wait_ge(k_copied, K_ITEMS * BRANCHES * GROUP)
            pe.wait_ge(shift_done, 1 + BRANCHES)
            emit.engine = pe
            stages(emit)


def kernel(x, ctx_2048, L0_xattn_Wq, L0_xattn_Wk, L0_xattn_Wv, L0_xattn_Wk_ip, L0_xattn_Wv_ip, L0_xattn_Wo, L0_xattn_bo):
    import concourse.bacc as bacc
    from concourse.bass_utils import run_bass_kernel_spmd

    def chunked(w):
        w = np.asarray(w)
        return np.ascontiguousarray(w.T.reshape(w.shape[1] // P, P, w.shape[0]).transpose(1, 0, 2)).reshape(P, -1)

    x = np.asarray(x)
    ctx = np.asarray(ctx_2048)
    arrays = {
        "x_in": np.ascontiguousarray(x.reshape(BATCHES, STEPS, N, GROUPS, P).transpose(1, 0, 4, 3, 2)),
        "ctx_in": np.ascontiguousarray(ctx.reshape(BATCHES, BRANCHES, KEYS, CTX_CHUNKS, P).transpose(4, 3, 1, 0, 2)),
        "wq_in": chunked(L0_xattn_Wq),
        "wk_in": np.stack([chunked(L0_xattn_Wk), chunked(L0_xattn_Wk_ip)]),
        "wv_in": np.stack([chunked(L0_xattn_Wv), chunked(L0_xattn_Wv_ip)]),
        "wo_in": chunked(L0_xattn_Wo),
        "bo_in": np.ascontiguousarray(np.asarray(L0_xattn_bo).reshape(GROUPS, P).T),
    }
    nc = bacc.Bacc("TRN2", target_bir_lowering=False, num_devices=1)
    args = [nc.dram_tensor(name, a.shape, mybir.dt.from_np(a.dtype), kind="ExternalInput").ap()
            for name, a in arrays.items()]
    out = nc.dram_tensor("y_out", (STEPS, BATCHES, P, GROUPS, N), F32, kind="ExternalOutput").ap()
    build(nc, *args, out)
    y = run_bass_kernel_spmd(nc, [arrays], core_ids=[0]).results[0]["y_out"]
    return np.ascontiguousarray(y.transpose(1, 0, 4, 3, 2)).reshape(BATCHES, SEQ, C)
```

```python
from contextlib import ExitStack

import numpy as np

import concourse.bass as bass
from concourse import mybir

ACT = mybir.ActivationFunctionType
ALU = mybir.AluOpType
AXIS = mybir.AxisListType
F32 = mybir.dt.float32
F32R = mybir.dt.float32r

P = 128
BATCHES, SEQ, C, CTX_C = 2, 2048, 640, 1024
HEADS, KEYS, BRANCHES = 20, 77, 2
D = C // HEADS
SCALE = float(np.float32(1.0) / np.sqrt(np.float32(D)))
GROUP = P // D
GROUPS = C // P
CTX_CHUNKS = CTX_C // P
N = 256
SUB = N // P
TILES = BATCHES * SEQ // N
STEPS = TILES // BATCHES
UNITS = TILES * GROUPS
BLK = GROUP * KEYS
SHIFT_ROW = 3 * D
STACK = SHIFT_ROW + BRANCHES
PASSES = 3
STEPS_OF_PRODUCT = PASSES * GROUPS
MAXES = SUB * BRANCHES
A_ITEMS = MAXES + 1
SPREAD_LAG = 5
OUT_LAG = 10
HALF = D // 2
WARM_UP = 7
PIECES = [(0, 1), (1, 2), (2, 4), (4, 6), (6, 8)]
DMA = 16


class Unit:

    def __init__(self, t, c):
        carry, c = divmod(c, GROUPS * BATCHES)
        self.t, self.c = t + carry, c
        self.batch, self.g = divmod(c, GROUPS)
        self.slot = c % 2
        self.fixed = isinstance(self.t, int)

    def plus(self, k):
        return Unit(self.t, self.c + k)

    def tile_plus(self, k):
        return Unit(self.t, self.c - self.g + k * GROUPS)

    def number(self, scale=1, plus=0):
        return self.t * (GROUPS * BATCHES * scale) + (self.c * scale + plus)

    def tile(self, scale=1, plus=0):
        return self.t * (BATCHES * scale) + (self.batch * scale + plus)

    def uses_of_slot(self, scale=1):
        return self.t * (GROUPS * BATCHES // 2 * scale) + (self.c // 2 + 1) * scale

    def exists(self):
        return not self.fixed or 0 <= self.t < STEPS


def wait(eng, sem, value):
    if not isinstance(value, int) or value > 0:
        eng.wait_ge(sem, value)


def build(nc, x_d, ctx_d, wq_d, wk_d, wv_d, wo_d, bo_d, out_d):
    with ExitStack() as stack:
        def sbuf(name, shape, dt=F32, scope=stack):
            return scope.enter_context(nc.sbuf_tensor(name, shape, dt))

        def psum(name):
            return stack.enter_context(nc.psum_tensor(name, [P, 512], F32))

        def sem(name):
            return stack.enter_context(nc.semaphore(name))

        wq_hi = sbuf("wq_hi", [P, GROUPS, C], F32R)
        wo_hi = sbuf("wo_hi", [P, GROUPS, C], F32R)
        with ExitStack() as raw:
            wq_raw = sbuf("wq_raw", [P, GROUPS, C], scope=raw)
            wo_raw = sbuf("wo_raw", [P, GROUPS, C], scope=raw)
        wq_lo = sbuf("wq_lo", [P, GROUPS, C], F32R)
        wo_lo = sbuf("wo_lo", [P, GROUPS, C], F32R)
        k_stack = sbuf("k_stack", [P, BRANCHES, HEADS, BATCHES, KEYS], F32R)
        k_diag = sbuf("k_diag", [P, BRANCHES, GROUPS, BATCHES, GROUP, KEYS], F32R)
        v = sbuf("v", [P, BRANCHES, BATCHES, C])
        bo = sbuf("bo", [P, GROUPS])
        ident = sbuf("ident", [P, P])
        sum_first = sbuf("sum_first", [P, D])
        sum_one = sbuf("sum_one", [P, 2 * D])
        low_rows = sbuf("low_rows", [P, 1])
        spread = sbuf("spread", [P, BRANCHES * GROUPS, GROUP, D], F32R)
        x_raw = sbuf("x_raw", [P, GROUPS, N])
        x_hi = sbuf("x_hi", [P, BATCHES, GROUPS, N], F32R)
        x_lo = sbuf("x_lo", [P, BATCHES, GROUPS, N], F32R)
        q_hi = sbuf("q_hi", [P, 2, N], F32R)
        q_stack = sbuf("q_stack", [P, 2, GROUP, N], F32R)
        row_max = sbuf("row_max", [P, 2, BRANCHES, GROUP, SUB])
        max_rows = sbuf("max_rows", [BRANCHES * SUB * GROUP, 2, P], F32R)
        with ExitStack() as before:
            stage = [sbuf(f"stage{i}", [P, CTX_CHUNKS * C], scope=before) for i in range(BRANCHES)]
            ctx = sbuf("ctx", [P, BRANCHES, CTX_CHUNKS, BATCHES, KEYS], scope=before)
        probs = sbuf("probs", [P, GROUP, BRANCHES * N])
        scaled = sbuf("scaled", [P, 2, BRANCHES * N])
        attn_hi = sbuf("attn_hi", [P, BATCHES, GROUPS, N], F32R)
        pv_sb = sbuf("pv_sb", [P, GROUPS, BRANCHES * N])
        attn_lo = sbuf("attn_lo", [P, BATCHES, GROUPS, N], F32R)
        res = sbuf("res", [P, GROUPS, N])
        inv = sbuf("inv", [P, N])
        inv_hi = sbuf("inv_hi", [P, N], F32R)
        inv_parts = sbuf("inv_parts", [P, N], F32R)
        y = sbuf("y", [P, 2, N])
        v_chan = [stage[0][:, (GROUP + 2) * BRANCHES * N + br * GROUPS * BATCHES * KEYS:][:, 0:GROUPS * BATCHES * KEYS]
                  .rearrange("p (g n) -> p g n", g=GROUPS) for br in range(BRANCHES)]

        q_ps = psum("q_ps")
        x_ps = psum("x_ps")
        a_ps = [psum("a_ps0"), psum("a_ps1")]
        b_ps = [psum("b_ps0"), psum("b_ps1")]
        pv_ps = psum("pv_ps")
        sum_ps = psum("sum_ps")

        x_loaded = sem("x_loaded")
        wq_loaded, wo_loaded = sem("wq_loaded"), sem("wo_loaded")
        bo_loaded = sem("bo_loaded")
        ctx_loaded = [[sem(f"ctx_loaded{br}_{n}") for n in range(len(PIECES))] for br in range(BRANCHES)]
        wk_loaded = [[sem(f"wk_loaded{br}_{n}") for n in range(len(PIECES))] for br in range(BRANCHES)]
        wv_loaded = [[sem(f"wv_loaded{br}_{n}") for n in range(len(PIECES))] for br in range(BRANCHES)]
        wq_hi_done, wq_lo_done = sem("wq_hi_done"), sem("wq_lo_done")
        wo_hi_done, wo_lo_done = sem("wo_hi_done"), sem("wo_lo_done")
        zeroed = sem("zeroed")
        consts = sem("consts")
        low_rows_done = sem("low_rows_done")
        shift_done = sem("shift_done")
        rows_picked = sem("rows_picked")
        k_acc = sem("k_acc")
        k_hi_done = sem("k_hi_done")
        k_lo_done = sem("k_lo_done")
        k_copied = [sem(f"k_copied{n}") for n in range(2)]
        v_acc = sem("v_acc")
        v_kept = [sem(f"v_kept{n}") for n in range(2)]
        v_turned = sem("v_turned")
        v_done = [sem(f"v_done{n}") for n in range(2)]
        v_zeroed = sem("v_zeroed")
        probs_zeroed = sem("probs_zeroed")
        x_hi_done, x_lo_done = sem("x_hi_done"), sem("x_lo_done")
        q_acc = sem("q_acc")
        q_hi_done = sem("q_hi_done")
        q_top_done = sem("q_top_done")
        q_low_done = sem("q_low_done")
        q_third = [sem(f"q_third{s}") for s in range(2)]
        a_ready, a_drained = sem("a_ready"), sem("a_drained")
        max_in = [sem(f"max_in{s}") for s in range(2)]
        b_ready, b_drained = sem("b_ready"), sem("b_drained")
        pv_ready = sem("pv_ready")
        pv_drained = sem("pv_drained")
        inv_done = sem("inv_done")
        sums_kept = sem("sums_kept")
        inv_spread = sem("inv_spread")
        out_ready = sem("out_ready")
        scaled_done = sem("scaled_done")
        y_done = sem("y_done")
        y_added = sem("y_added")
        last_added = sem("last_added")
        attn_done = sem("attn_done")
        attn_hi_done, attn_lo_done = sem("attn_hi_done"), sem("attn_lo_done")
        res_loaded = [sem(f"res_loaded{m}") for m in range(GROUPS)]
        stored = sem("stored")

        INV_STEPS = 3
        K_ITEMS = BRANCHES * GROUPS
        k_banks = [a_ps, b_ps]
        v_banks = [[pv_ps, sum_ps], b_ps]
        turn_banks = [x_ps, pv_ps, sum_ps]

        def group_cols(g):
            return slice(g // 2 * BATCHES * KEYS, (g // 2 + 1) * BATCHES * KEYS)

        LAST = Unit(STEPS - 1, GROUPS)
        last_out = [x_ps, pv_ps, x_ps, pv_ps, x_ps, *a_ps, *b_ps, q_ps]
        LAST_CHUNKS = [LAST.plus(m) for m in range(-GROUPS, GROUPS)]

        def last_place(c):
            return x_raw[:, c.g, :] if c.number() >= LAST.number() else res[:, c.g, :]

        block = stack.enter_context(nc.Block())

        def stages(emit):
            def pair(t):
                for c in range(GROUPS * BATCHES):
                    emit(Unit(t, c))
            pair(0)
            with emit.engine.Fori(1, STEPS - 1) as t:
                pair(t)
            pair(STEPS - 1)

        @block.sync
        def _(sp):
            def pieces(weights, br, loaded, parts=range(len(PIECES)), with_ctx=False):
                w = stage[br][:].rearrange("p (k c) -> p k c", k=CTX_CHUNKS)
                for n in parts:
                    first, end = PIECES[n]
                    if with_ctx:
                        sp.dma_start(ctx[:, br, first:end], ctx_d[:, br, first:end]).then_inc(ctx_loaded[br][n], DMA)
                    sp.dma_start(w[:, first:end], weights[br, :, first:end]).then_inc(loaded[br][n], DMA)

            pieces(wk_d, 0, wk_loaded, with_ctx=True)
            pieces(wk_d, 1, wk_loaded, with_ctx=True)
            sp.wait_ge(k_acc, 1)
            pieces(wv_d, 0, wv_loaded, range(3))
            sp.dma_start(wq_raw[:], wq_d).then_inc(wq_loaded, DMA)
            pieces(wv_d, 0, wv_loaded, range(3, 4))
            sp.dma_start(x_raw[:], x_d[0, 0]).then_inc(x_loaded, DMA)
            pieces(wv_d, 0, wv_loaded, range(4, len(PIECES)))
            sp.dma_start(bo[:], bo_d).then_inc(bo_loaded, DMA)
            sp.wait_ge(k_acc, 2)
            pieces(wv_d, 1, wv_loaded)
            sp.dma_start(wo_raw[:], wo_d).then_inc(wo_loaded, DMA)
            sp.wait_ge(x_lo_done, 1)
            sp.dma_start(x_raw[:], x_d[0, 1]).then_inc(x_loaded, DMA)

            def maxima(u):
                wait(sp, a_drained, u.number(A_ITEMS, A_ITEMS))
                sp.dma_start(q_stack[SHIFT_ROW:STACK, u.slot].bitcast(F32),
                             max_rows[:, u.slot, :].bitcast(F32)).then_inc(max_in[u.slot], DMA)

            def store(c):
                wait(sp, y_added, c.number(1, 1))
                sp.dma_start(out_d[c.t, c.batch, :, c.g, :], res[:, c.g, :]).then_inc(stored, DMA)

            def load_residual(c):
                wait(sp, stored, c.number(DMA, (1 - GROUPS) * DMA))
                if c.fixed and c.number() == 0:
                    sp.wait_ge(v_acc, BRANCHES)
                sp.dma_start(res[:, c.g, :], x_d[c.t, c.batch, :, c.g, :]).then_inc(res_loaded[c.g], DMA)

            def third_block(u):
                wait(sp, q_top_done, u.number(1, 1))
                sp.dma_start(q_stack[2 * D:3 * D, u.slot].bitcast(F32),
                             q_stack[0:D, u.slot].bitcast(F32)).then_inc(q_third[u.slot], DMA)

            def emit(u):
                ahead = u.tile_plus(2)
                if u.plus(1).exists():
                    maxima(u.plus(1))
                if u.plus(2).exists():
                    third_block(u.plus(2))
                if u.plus(-OUT_LAG).exists():
                    store(u.plus(-OUT_LAG))
                if u.plus(GROUPS - OUT_LAG).exists():
                    load_residual(u.plus(GROUPS - OUT_LAG))
                if u.g == 2 and ahead.exists():
                    wait(sp, x_lo_done, u.tile(1, 2))
                    sp.dma_start(x_raw[:], x_d[ahead.t, ahead.batch]).then_inc(x_loaded, DMA)

            third_block(Unit(0, 0))
            maxima(Unit(0, 0))
            third_block(Unit(0, 1))
            emit.engine = sp
            stages(emit)
            for n, c in enumerate(LAST_CHUNKS):
                sp.wait_ge(last_added, n + 1)
                sp.dma_start(out_d[c.t, c.batch, :, c.g, :], last_place(c)).then_inc(stored, DMA)
            sp.wait_ge(stored, TILES * GROUPS * DMA)

        @block.gpsimd
        def _(pool):
            nc.gpsimd.memset(ident[:], 0.0).then_inc(consts, 1)
            pool.wait_ge(consts, 1)
            nc.gpsimd.affine_select(out=ident[:], in_=ident[:], compare_op=ALU.not_equal, fill=1.0, base=0,
                                    pattern=[[-1, P]], channel_multiplier=1).then_inc(consts, 1)
            nc.gpsimd.memset(sum_one[:], 0.0).then_inc(consts, 1)
            nc.gpsimd.memset(sum_first[:], 1.0).then_inc(consts, 1)
            pool.wait_ge(consts, 4)
            nc.gpsimd.memset(sum_one[:, D - 1:2 * D:HALF], 1.0).then_inc(consts, 1)
            for c in (0, HALF):
                nc.gpsimd.memset(sum_first[:, c + 1:c + BRANCHES * GROUPS], 0.0).then_inc(consts, 1)
            nc.gpsimd.memset(k_diag[:, 1].bitcast(F32), 0.0).then_inc(zeroed, 1)
            nc.gpsimd.memset(spread[:].bitcast(F32), 0.0).then_inc(consts, 1)
            for step, row in enumerate((0, HALF)):
                pool.wait_ge(consts, 8 + step)
                nc.gpsimd.affine_select(out=spread[:], in_=spread[:], compare_op=ALU.not_equal, fill=1.0, base=-row,
                                        pattern=[[-1, BRANCHES * GROUPS], [-D, GROUP], [0, D]],
                                        channel_multiplier=1).then_inc(consts, 1)

            def split_x(u):
                wait(pool, x_hi_done, u.tile(1, 1))
                nc.gpsimd.tensor_tensor(x_lo[:, u.batch], x_raw[:], x_hi[:, u.batch].bitcast(F32),
                                        ALU.subtract).then_inc(x_lo_done, 1)

            def add_branches(u):
                wait(pool, scaled_done, u.number(1, 1))
                s = u.slot
                nc.gpsimd.tensor_tensor(scaled[:, s, 0:N], scaled[:, s, 0:N], scaled[:, s, N:2 * N],
                                        ALU.add).then_inc(attn_done, 1)

            def attn_low(u):
                wait(pool, attn_hi_done, u.number(1, 1))
                nc.gpsimd.tensor_tensor(attn_lo[:, u.batch, u.g, :], scaled[:, u.slot, 0:N],
                                        attn_hi[:, u.batch, u.g, :].bitcast(F32), ALU.subtract).then_inc(attn_lo_done, 1)

            def add_residual(c):
                wait(pool, y_done, c.number(1, 1))
                wait(pool, res_loaded[c.g], c.tile(DMA, DMA))
                nc.gpsimd.tensor_tensor(res[:, c.g, :], y[:, c.slot, :], res[:, c.g, :], ALU.add).then_inc(y_added, 1)

            def emit(u):
                ahead, norm, chunk = u.tile_plus(1), u.plus(-1 - SPREAD_LAG), u.plus(-OUT_LAG)
                if norm.exists():
                    add_branches(norm)
                    attn_low(norm)
                if u.g == 1 and ahead.exists() and not (u.fixed and u.number() == 1):
                    split_x(ahead)
                if chunk.exists():
                    add_residual(chunk)

            split_x(Unit(0, 0))
            split_x(Unit(0, GROUPS))
            emit.engine = pool
            stages(emit)
            add_branches(LAST.plus(-1))
            attn_low(LAST.plus(-1))
            add_branches(LAST)
            for g in range(GROUPS):
                if g + 1 < GROUPS:
                    add_branches(LAST.plus(g + 1))
                attn_low(LAST.plus(g))

        @block.scalar
        def _(act):
            def q_high(u):
                wait(act, q_acc, u.number(1, 1))
                wait(act, a_ready, u.number(A_ITEMS, -A_ITEMS))
                wait(act, q_low_done, u.number(1, -1))
                nc.scalar.activation(q_hi[:, u.slot, :], q_ps[:, 0:N], ACT.Copy).then_inc(q_hi_done, 1)

            def q_top(u):
                wait(act, b_ready, u.number(GROUP, -GROUP))
                wait(act, q_hi_done, u.number(1, 1))
                for j in range(GROUP):
                    done = nc.scalar.activation(q_stack[0:D, u.slot, j, :],
                                                q_hi[j * D:(j + 1) * D, u.slot, :].bitcast(F32), ACT.Copy)
                done.then_inc(q_top_done, 1)

            def exp(u, j):
                wait(act, b_ready, u.number(GROUP, j + 1))
                if j == 0:
                    wait(act, pv_ready, u.number())
                nc.scalar.activation(probs[0:KEYS, j, :], b_ps[j % 2][0:KEYS, :], ACT.Exp).then_inc(b_drained, 1)

            def keep_pv(u):
                wait(act, pv_ready, u.number(1, 1))
                wait(act, scaled_done, u.number(1, 1 - SPREAD_LAG))
                nc.scalar.activation(pv_sb[:, u.g, :], pv_ps[:], ACT.Copy).then_inc(pv_drained, 1)

            def split_x(u):
                wait(act, x_loaded, u.tile(DMA, DMA))
                wait(act, q_acc, u.number(1, -GROUPS))
                nc.scalar.activation(x_hi[:, u.batch], x_raw[:], ACT.Copy).then_inc(x_hi_done, 1)

            def keep_sums(u):
                wait(act, pv_ready, u.number(1, GROUPS))
                wait(act, inv_done, u.tile(INV_STEPS))
                nc.scalar.activation(inv[:], sum_ps[:, 0:N], ACT.Copy).then_inc(sums_kept, 1)

            def add_bias(c):
                wait(act, out_ready, c.number(1, 1))
                nc.scalar.activation(y[:, c.slot, :], x_ps[:, 0:N], ACT.Identity, bias=bo[:, c.g:c.g + 1]).then_inc(y_done, 1)

            def attn_high(u):
                wait(act, attn_done, u.number(1, 1))
                nc.scalar.activation(attn_hi[:, u.batch, u.g, :], scaled[:, u.slot, 0:N], ACT.Copy).then_inc(attn_hi_done, 1)

            def emit(u):
                before, ahead, nxt = u.tile_plus(-1), u.tile_plus(2), u.plus(2)
                norm, chunk = u.plus(-1 - SPREAD_LAG), u.plus(-OUT_LAG)
                exp(u, 0)
                exp(u, 1)
                if u.plus(-1).exists():
                    keep_pv(u.plus(-1))
                if u.g == 0 and before.exists():
                    keep_sums(before)
                exp(u, 2)
                if norm.exists():
                    attn_high(norm)
                exp(u, 3)
                if nxt.exists():
                    q_high(nxt)
                    q_top(nxt)
                if chunk.exists():
                    add_bias(chunk)
                if u.g == GROUPS - 1 and ahead.exists():
                    split_x(ahead)
                if u.fixed and u.number() == 0:
                    split_x(Unit(0, GROUPS))
                if u.fixed and u.number() in range(GROUPS):
                    weight_high(wo_hi[:, u.g], wo_raw[:, u.g], wo_loaded, wo_hi_done)

            def weight_high(hi, raw, loaded, done):
                act.wait_ge(loaded, DMA)
                nc.scalar.activation(hi, raw, ACT.Copy).then_inc(done, 1)

            def keys_high(item):
                br, g = divmod(item, GROUPS)
                act.wait_ge(k_acc, br + 1)
                if g >= 2:
                    act.wait_ge(k_lo_done, item - 1)
                for j in range(GROUP):
                    rows = slice(j * D, (j + 1) * D)
                    done = nc.scalar.activation(
                        k_diag[rows, br, g, :, j, :],
                        k_banks[br][g % 2][rows, group_cols(g)].rearrange("p (b n) -> p b n", b=BATCHES),
                        ACT.Copy, scale=SCALE)
                done.then_inc(k_hi_done, 1)

            def keys_top(item):
                br, g = divmod(item, GROUPS)
                act.wait_ge(k_hi_done, item + 1)
                for j in range(GROUP):
                    nc.scalar.activation(k_stack[0:D, br, g * GROUP + j],
                                         k_diag[j * D:(j + 1) * D, br, g, :, j, :].bitcast(F32),
                                         ACT.Copy).then_inc(k_copied[0], 1)

            def keep_v(br):
                act.wait_ge(v_acc, br + 1)
                nc.scalar.activation(v_chan[br][:, 0::2],
                                     v_banks[br][0][:, 0:3 * BATCHES * KEYS].rearrange("p (g n) -> p g n", g=3),
                                     ACT.Copy).then_inc(v_kept[0], 1)

            def place_v(item):
                br, g = divmod(item, GROUPS)
                act.wait_ge(v_turned, item + 1)
                nc.scalar.activation(v[0:KEYS, br, :, g * P:(g + 1) * P],
                                     turn_banks[item % 3][0:KEYS, 0:BATCHES * P].rearrange("p (b c) -> p b c", b=BATCHES),
                                     ACT.Copy).then_inc(v_done[0], 1)

            act.wait_ge(consts, 2)
            act.wait_ge(shift_done, 1)
            for br in range(BRANCHES):
                nc.scalar.activation(k_stack[SHIFT_ROW:STACK, br], k_stack[SHIFT_ROW:STACK, br].bitcast(F32), ACT.Copy,
                                     scale=ident[SHIFT_ROW:STACK, SHIFT_ROW + br:SHIFT_ROW + br + 1]).then_inc(rows_picked, 1)
            act.wait_ge(zeroed, 2)
            text_items, ip_items = range(GROUPS), range(GROUPS, K_ITEMS)
            for item in text_items:
                keys_high(item)
            for item in text_items:
                keys_top(item)
            for item in ip_items:
                keys_high(item)
            weight_high(wq_hi[:], wq_raw[:], wq_loaded, wq_hi_done)
            split_x(Unit(0, 0))
            for item in ip_items:
                keys_top(item)
            keep_v(0)
            q_high(Unit(0, 0))
            q_top(Unit(0, 0))
            act.wait_ge(v_zeroed, 1)
            for item in range(0, GROUPS, 2):
                place_v(item)
            keep_v(1)
            q_high(Unit(0, 1))
            for item in range(GROUPS + 1, K_ITEMS, 2):
                place_v(item)
            q_top(Unit(0, 1))
            act.wait_ge(probs_zeroed, 1)
            act.wait_ge(bo_loaded, DMA)
            emit.engine = act
            stages(emit)
            keep_pv(LAST.plus(GROUPS - 1))
            keep_sums(LAST)
            for g in range(-1, GROUPS):
                attn_high(LAST.plus(g))

        @block.vector
        def _(dve):
            nc.vector.memset(k_diag[:, 0].bitcast(F32), 0.0).then_inc(zeroed, 1)
            nc.vector.memset(k_stack[SHIFT_ROW:STACK].bitcast(F32), -1.0).then_inc(shift_done, 1)
            nc.vector.memset(v[64:P], 0.0).then_inc(v_zeroed, 1)
            dve.wait_ge(consts, 2)
            nc.vector.tensor_reduce(low_rows[:], ident[:].rearrange("p (j d) -> p j d", j=GROUP)[:, :, HALF:], AXIS.XY,
                                    ALU.add, negate=True).then_inc(low_rows_done, 1)

            def weight_low(hi, raw, lo, hi_done, count, done):
                dve.wait_ge(hi_done, count)
                nc.vector.tensor_tensor(lo, raw, hi.bitcast(F32), ALU.subtract).then_inc(done, 1)

            def q_low(u):
                wait(dve, q_hi_done, u.number(1, 1))
                wait(dve, b_ready, u.number(GROUP, -GROUP))
                for j in range(GROUP):
                    rows = slice(j * D, (j + 1) * D)
                    done = nc.vector.tensor_tensor(q_stack[D:2 * D, u.slot, j, :], q_ps[rows, 0:N],
                                                   q_hi[rows, u.slot, :].bitcast(F32), ALU.subtract)
                done.then_inc(q_low_done, 1)

            def max_piece(u, k):
                sub, br = divmod(k, BRANCHES)
                wait(dve, a_ready, u.number(A_ITEMS, k + 1))
                bank = a_ps[(u.c * A_ITEMS + k) % 2]
                nc.vector.tensor_reduce(row_max[:, u.slot, br, :, sub],
                                        bank[:, 0:BLK].rearrange("p (j n) -> p j n", j=GROUP), AXIS.X,
                                        ALU.max).then_inc(a_drained, 1)

            def max_turned(u):
                wait(dve, a_ready, u.number(A_ITEMS, A_ITEMS))
                wait(dve, max_in[u.slot], u.uses_of_slot(DMA) - DMA)
                nc.vector.tensor_copy(max_rows[:, u.slot, :],
                                      a_ps[(u.c * A_ITEMS + MAXES) % 2][0:BRANCHES * SUB * GROUP, 0:P]).then_inc(a_drained, 1)

            def invert_sums(u):
                wait(dve, sums_kept, u.tile(1, 1))
                nc.vector.reciprocal(inv[:], inv[:]).then_inc(inv_done, 1)
                wait(dve, inv_spread, u.number())
                wait(dve, inv_done, u.tile(INV_STEPS, 1))
                nc.vector.tensor_copy(inv_hi[:], inv[:]).then_inc(inv_done, 1)
                wait(dve, inv_done, u.tile(INV_STEPS, 2))
                nc.vector.scalar_tensor_tensor(out=inv_parts[:], in0=inv_hi[:].bitcast(F32), scalar=low_rows[:],
                                               in1=inv[:], op0=ALU.mult, op1=ALU.add).then_inc(inv_done, 1)

            def normalise(u, bank=x_ps):
                wait(dve, inv_spread, u.number(1, 1))
                wait(dve, pv_drained, u.number(1, 1))
                wait(dve, attn_lo_done, u.number(1, -1))
                nc.vector.tensor_tensor(scaled[:, u.slot, :], bank[:], pv_sb[:, u.g, :],
                                        ALU.mult).then_inc(scaled_done, 1)

            def finish_last(n):
                c = LAST_CHUNKS[n]
                dve.wait_ge(out_ready, c.number(1, 1))
                if c.number() < LAST.number():
                    dve.wait_ge(res_loaded[c.g], c.tile(DMA, DMA))
                nc.vector.scalar_tensor_tensor(out=last_place(c), in0=last_out[n][:, 0:N], scalar=bo[:, c.g:c.g + 1],
                                               in1=last_place(c), op0=ALU.add, op1=ALU.add).then_inc(last_added, 1)

            def emit(u):
                norm, nxt = u.plus(-1 - SPREAD_LAG), u.plus(1)
                if norm.exists():
                    normalise(norm)
                if nxt.exists():
                    for k in range(MAXES):
                        max_piece(nxt, k)
                    max_turned(nxt)
                if u.g == 0 and u.tile_plus(-1).exists():
                    invert_sums(u.tile_plus(-1))
                if u.plus(2).exists():
                    q_low(u.plus(2))
                if u.fixed and u.number() in range(GROUPS):
                    weight_low(wo_hi[:, u.g], wo_raw[:, u.g], wo_lo[:, u.g], wo_hi_done, u.g + 1, wo_lo_done)

            def keys_low(item):
                br, g = divmod(item, GROUPS)
                dve.wait_ge(k_hi_done, item + 1)
                for j in range(GROUP):
                    rows = slice(j * D, (j + 1) * D)
                    done = nc.vector.scalar_tensor_tensor(
                        out=k_stack[2 * D:3 * D, br, g * GROUP + j],
                        in0=k_banks[br][g % 2][rows, group_cols(g)].rearrange("p (b n) -> p b n", b=BATCHES),
                        scalar=SCALE, in1=k_diag[rows, br, g, :, j, :].bitcast(F32), op0=ALU.mult, op1=ALU.subtract)
                done.then_inc(k_lo_done, 1)

            def keys_second(item):
                br, g = divmod(item, GROUPS)
                for j in range(GROUP):
                    nc.vector.tensor_copy(k_stack[D:2 * D, br, g * GROUP + j],
                                          k_diag[j * D:(j + 1) * D, br, g, :, j, :].bitcast(F32)).then_inc(k_copied[1], 1)

            def keep_v(br):
                dve.wait_ge(v_acc, br + 1)
                nc.vector.tensor_copy(v_chan[br][:, 1::2],
                                      v_banks[br][1][:, 0:2 * BATCHES * KEYS].rearrange("p (g n) -> p g n", g=2)
                                      ).then_inc(v_kept[1], 1)

            def place_v(item):
                br, g = divmod(item, GROUPS)
                dve.wait_ge(v_turned, item + 1)
                nc.vector.tensor_copy(v[0:KEYS, br, :, g * P:(g + 1) * P],
                                      turn_banks[item % 3][0:KEYS, 0:BATCHES * P].rearrange("p (b c) -> p b c", b=BATCHES)
                                      ).then_inc(v_done[1], 1)

            text_items, ip_items = range(GROUPS), range(GROUPS, K_ITEMS)
            for item in text_items:
                keys_low(item)
            for item in text_items:
                keys_second(item)
            for item in ip_items:
                keys_low(item)
            weight_low(wq_hi[:], wq_raw[:], wq_lo[:], wq_hi_done, 1, wq_lo_done)
            for item in ip_items:
                keys_second(item)
            keep_v(0)
            q_low(Unit(0, 0))
            nc.vector.memset(probs[64:P], 0.0).then_inc(probs_zeroed, 1)
            for k in range(MAXES):
                max_piece(Unit(0, 0), k)
            dve.wait_ge(v_zeroed, 1)
            max_turned(Unit(0, 0))
            for item in range(1, GROUPS, 2):
                place_v(item)
            keep_v(1)
            place_v(GROUPS)
            q_low(Unit(0, 1))
            for item in range(GROUPS + 2, K_ITEMS, 2):
                place_v(item)
            dve.wait_ge(bo_loaded, DMA)
            dve.wait_ge(low_rows_done, 1)
            emit.engine = dve
            stages(emit)
            normalise(LAST.plus(-1))
            invert_sums(LAST)
            finish_last(0)
            normalise(LAST, sum_ps)
            for n in (1, 2):
                finish_last(n)
            for g in (1, 2, 3):
                normalise(LAST.plus(g), sum_ps)
                if g + 2 < GROUPS:
                    finish_last(g + 2)
            normalise(LAST.plus(4), sum_ps)
            for n in range(GROUPS, 2 * GROUPS):
                finish_last(n)

        @block.tensor
        def _(pe):
            LAST_CHUNK = PASSES * (GROUPS - 1)

            def product_step(n, out, hi, lo, moving_hi, moving_lo):
                kind, k = divmod(n, GROUPS - 1) if n < LAST_CHUNK else (n - LAST_CHUNK, GROUPS - 1)
                return nc.tensor.matmul(out, (lo if kind == 1 else hi)(k), (moving_lo if kind == 2 else moving_hi)(k),
                                        start=(n == 0), stop=(n == STEPS_OF_PRODUCT - 1), skip_group_check=True)

            def project_q(u, first=0, end=STEPS_OF_PRODUCT):
                if not u.exists():
                    return
                cols = slice(u.g * P, (u.g + 1) * P)
                if first == 0:
                    if u.g == 0:
                        wait(pe, x_lo_done, u.tile(1, 1))
                    wait(pe, q_low_done, u.number())
                for n in range(first, end):
                    done = product_step(n, q_ps[:, 0:N], lambda k: wq_hi[:, k, cols], lambda k: wq_lo[:, k, cols],
                                        lambda k: x_hi[:, u.batch, k, :], lambda k: x_lo[:, u.batch, k, :])
                if end == STEPS_OF_PRODUCT:
                    done.then_inc(q_acc, 1)

            def max_scores(u, k):
                sub, br = divmod(k, BRANCHES)
                if k == 0:
                    wait(pe, q_hi_done, u.number(1, 1))
                wait(pe, a_drained, u.number(A_ITEMS, k - 1))
                nc.tensor.matmul(a_ps[(u.c * A_ITEMS + k) % 2][:, 0:BLK], q_hi[:, u.slot, sub * P:(sub + 1) * P],
                                 k_diag[:, br, u.g, u.batch].rearrange("p j n -> p (j n)"),
                                 start=True, stop=True).then_inc(a_ready, 1)

            def turn_maxima(u):
                wait(pe, a_drained, u.number(A_ITEMS, MAXES))
                nc.tensor.transpose(a_ps[(u.c * A_ITEMS + MAXES) % 2][0:BRANCHES * SUB * GROUP, 0:P],
                                    row_max[:, u.slot].rearrange("p r j s -> p (r j s)"), ident[:]).then_inc(a_ready, 1)

            def scores(u, j):
                if j == 0:
                    wait(pe, q_low_done, u.number(1, 1))
                    wait(pe, q_third[u.slot], u.uses_of_slot(DMA))
                    wait(pe, max_in[u.slot], u.uses_of_slot(DMA))
                wait(pe, b_drained, u.number(GROUP, j - 1))
                for br in range(BRANCHES):
                    done = nc.tensor.matmul(b_ps[j % 2][0:KEYS, br * N:(br + 1) * N],
                                            k_stack[0:STACK, br, u.g * GROUP + j, u.batch, :],
                                            q_stack[0:STACK, u.slot, j, :], start=True, stop=True)
                done.then_inc(b_ready, 1)

            def row_sums(u):
                wait(pe, b_drained, u.number(GROUP, GROUP))
                if u.g == 0:
                    wait(pe, sums_kept, u.tile())
                if u.fixed and u.number() == 0:
                    for n in range(2):
                        pe.wait_ge(v_done[n], K_ITEMS // 2)
                for br in range(BRANCHES):
                    c = BRANCHES * u.g + br
                    first = c == 0
                    for j in range(GROUP):
                        nc.tensor.matmul(sum_ps[j * D:(j + 1) * D, 0:N],
                                         sum_first[:] if first else sum_one[:, D - 1 - c:2 * D - 1 - c],
                                         probs[:, j, br * N:(br + 1) * N], start=first,
                                         stop=(c == BRANCHES * GROUPS - 1), skip_group_check=True)

            def weigh_values(u):
                wait(pe, pv_drained, u.number())
                for br in range(BRANCHES):
                    for j in range(GROUP):
                        h = u.g * GROUP + j
                        done = nc.tensor.matmul(pv_ps[j * D:(j + 1) * D, br * N:(br + 1) * N],
                                                v[:, br, u.batch, h * D:(h + 1) * D],
                                                probs[:, j, br * N:(br + 1) * N], start=True, stop=True)
                done.then_inc(pv_ready, 1)

            def spread_matmuls(u, bank):
                for br in range(BRANCHES):
                    sel = spread[:, BRANCHES * u.g + br].rearrange("p j d -> p (j d)")
                    done = nc.tensor.matmul(bank[:, br * N:(br + 1) * N], sel, inv_parts[:], start=True, stop=True)
                done.then_inc(inv_spread, 1)

            def spread_inverse(u):
                if u.g == 0:
                    wait(pe, inv_done, u.tile(INV_STEPS, INV_STEPS))
                wait(pe, scaled_done, u.number())
                wait(pe, y_done, u.number(1, 1 + SPREAD_LAG - OUT_LAG))
                spread_matmuls(u, x_ps)

            def project_out(c):
                wait(pe, scaled_done, c.number(1, OUT_LAG - SPREAD_LAG))
                out_chunk(c, x_ps)

            def out_chunk(c, bank):
                cols = slice(c.g * P, (c.g + 1) * P)
                for n in range(STEPS_OF_PRODUCT):
                    if c.g == 0 and n == 0:
                        wait(pe, attn_hi_done, c.number(1, GROUPS - 1))
                    if c.g == 0 and n == 2 * (GROUPS - 1):
                        wait(pe, attn_lo_done, c.number(1, GROUPS - 1))
                    if c.g == 0 and n == LAST_CHUNK:
                        wait(pe, attn_hi_done, c.number(1, GROUPS))
                    if c.g == 0 and n == STEPS_OF_PRODUCT - 1:
                        wait(pe, attn_lo_done, c.number(1, GROUPS))
                    done = product_step(n, bank[:, 0:N], lambda k: wo_hi[:, k, cols], lambda k: wo_lo[:, k, cols],
                                        lambda k: attn_hi[:, c.batch, k, :], lambda k: attn_lo[:, c.batch, k, :])
                done.then_inc(out_ready, 1)

            def end_last_tiles():
                def spread_last(g):
                    if g == 0:
                        pe.wait_ge(inv_done, LAST.tile(INV_STEPS, INV_STEPS))
                    else:
                        pe.wait_ge(scaled_done, LAST.number(1, g))
                    spread_matmuls(LAST.plus(g), sum_ps)

                def grow(k):
                    pe.wait_ge(attn_hi_done, LAST.number(1, k + 1))
                    chunks = [(bank[:, 0:N], slice(m * P, (m + 1) * P)) for m, bank in enumerate(last_out[GROUPS:])]
                    for out, cols in chunks:
                        for w in (wo_hi, wo_lo):
                            nc.tensor.matmul(out, w[:, k, cols], attn_hi[:, LAST.batch, k, :],
                                             start=(k == 0 and w is wo_hi), stop=False, skip_group_check=True)
                    pe.wait_ge(attn_lo_done, LAST.number(1, k + 1))
                    for out, cols in chunks:
                        done = nc.tensor.matmul(out, wo_hi[:, k, cols], attn_lo[:, LAST.batch, k, :], start=False,
                                                stop=(k == GROUPS - 1), skip_group_check=True)
                        if k == GROUPS - 1:
                            done.then_inc(out_ready, 1)

                def chunk(n):
                    if n == 0:
                        pe.wait_ge(scaled_done, LAST.number())
                    elif n == 1:
                        pe.wait_ge(pv_drained, UNITS)
                    else:
                        pe.wait_ge(last_added, n - 1)
                    out_chunk(LAST_CHUNKS[n], last_out[n])

                chunk(0)
                chunk(1)
                spread_last(0)
                chunk(2)
                spread_last(1)
                chunk(3)
                spread_last(2)
                grow(0)
                chunk(4)
                spread_last(3)
                grow(1)
                spread_last(4)
                for k in range(2, GROUPS):
                    grow(k)

            def emit(u):
                nxt, norm, chunk = u.plus(1), u.plus(-SPREAD_LAG), u.plus(-OUT_LAG)

                def find_max(k):
                    if nxt.exists():
                        max_scores(nxt, k) if k < MAXES else turn_maxima(nxt)

                find_max(0)
                find_max(1)
                scores(u, 0)
                scores(u, 1)
                project_q(u.plus(2), 0, 8)
                find_max(2)
                scores(u, 2)
                find_max(3)
                project_q(u.plus(2), 8, 10)
                scores(u, 3)
                project_q(u.plus(2), 10, 13)
                find_max(MAXES)
                project_q(u.plus(2), 13)
                if chunk.exists():
                    project_out(chunk)
                row_sums(u)
                if norm.exists() and norm.g > 0:
                    spread_inverse(norm)
                weigh_values(u)
                if norm.exists() and norm.g == 0:
                    spread_inverse(norm)
                if u.fixed and u.number() == OUT_LAG - 1:
                    pe.wait_ge(wo_lo_done, GROUPS)

            def project_ctx(banks, weights_loaded, br, chunks, done_sem):
                w = stage[br][:].rearrange("p (k c) -> p k c", k=CTX_CHUNKS)
                for k in chunks:
                    for n, (first, _) in enumerate(PIECES):
                        if k == first:
                            pe.wait_ge(ctx_loaded[br][n], DMA)
                            pe.wait_ge(weights_loaded[br][n], DMA)
                    for g in range(GROUPS):
                        done = nc.tensor.matmul(banks[g % 2][:, group_cols(g)], w[:, k, g * P:(g + 1) * P],
                                                ctx[:, br, k].rearrange("p b n -> p (b n)"), start=(k == 0 and g < 2),
                                                stop=(k == CTX_CHUNKS - 1), skip_group_check=True)
                    if k == CTX_CHUNKS - 1:
                        done.then_inc(done_sem, 1)

            def turn_v(item):
                br, g = divmod(item, GROUPS)
                pe.wait_ge(v_kept[g % 2], br + 1)
                if item >= 3:
                    pe.wait_ge(v_done[(item - 3) % 2], (item - 3) // 2 + 1)
                for b in range(BATCHES):
                    done = nc.tensor.transpose(turn_banks[item % 3][0:KEYS, b * P:(b + 1) * P],
                                               v_chan[br][:, g, b * KEYS:(b + 1) * KEYS], ident[:])
                done.then_inc(v_turned, 1)

            pe.wait_ge(consts, 2)
            for _ in range(WARM_UP):
                nc.tensor.matmul(x_ps[:, 0:P], ident[:], ident[:], start=True, stop=True)
            for br in range(BRANCHES):
                project_ctx(k_banks[br], wk_loaded, br, range(CTX_CHUNKS), k_acc)
            project_ctx(v_banks[0], wv_loaded, 0, range(CTX_CHUNKS), v_acc)
            pe.wait_ge(k_lo_done, K_ITEMS)
            pe.wait_ge(consts, 10)
            first = Unit(0, 0)

            def project_ip_values(first_chunk, end):
                project_ctx(v_banks[1], wv_loaded, 1, range(first_chunk, end), v_acc)

            project_ip_values(0, 1)
            pe.wait_ge(wq_lo_done, 1)
            project_q(first)
            project_ip_values(1, 4)
            max_scores(first, 0)
            max_scores(first, 1)
            project_ip_values(4, 5)
            max_scores(first, 2)
            max_scores(first, 3)
            project_ip_values(5, 6)
            turn_maxima(first)
            turn_v(0)
            turn_v(1)
            project_ip_values(6, 7)
            for item in range(2, GROUPS):
                turn_v(item)
            project_ip_values(7, CTX_CHUNKS)
            project_q(first.plus(1))
            for item in range(GROUPS, K_ITEMS):
                turn_v(item)
            for n in range(2):
                pe.wait_ge(k_copied[n], K_ITEMS * GROUP)
            pe.wait_ge(rows_picked, BRANCHES)
            emit.engine = pe
            stages(emit)
            end_last_tiles()


def kernel(x, ctx_2048, L0_xattn_Wq, L0_xattn_Wk, L0_xattn_Wv, L0_xattn_Wk_ip, L0_xattn_Wv_ip, L0_xattn_Wo, L0_xattn_bo):
    import concourse.bacc as bacc
    from concourse.bass_utils import run_bass_kernel_spmd

    def chunked(w):
        w = np.asarray(w)
        return np.ascontiguousarray(w.T.reshape(w.shape[1] // P, P, w.shape[0]).transpose(1, 0, 2))

    x = np.asarray(x)
    ctx = np.asarray(ctx_2048)
    arrays = {
        "x_in": np.ascontiguousarray(x.reshape(BATCHES, STEPS, N, GROUPS, P).transpose(1, 0, 4, 3, 2)),
        "ctx_in": np.ascontiguousarray(ctx.reshape(BATCHES, BRANCHES, KEYS, CTX_CHUNKS, P).transpose(4, 1, 3, 0, 2)),
        "wq_in": chunked(L0_xattn_Wq),
        "wk_in": np.stack([chunked(L0_xattn_Wk), chunked(L0_xattn_Wk_ip)]),
        "wv_in": np.stack([chunked(L0_xattn_Wv), chunked(L0_xattn_Wv_ip)]),
        "wo_in": chunked(L0_xattn_Wo),
        "bo_in": np.ascontiguousarray(np.asarray(L0_xattn_bo).reshape(GROUPS, P).T),
    }
    nc = bacc.Bacc("TRN2", target_bir_lowering=False, num_devices=1)
    args = [nc.dram_tensor(name, a.shape, mybir.dt.from_np(a.dtype), kind="ExternalInput").ap()
            for name, a in arrays.items()]
    out = nc.dram_tensor("y_out", (STEPS, BATCHES, P, GROUPS, N), F32, kind="ExternalOutput").ap()
    build(nc, *args, out)
    y = run_bass_kernel_spmd(nc, [arrays], core_ids=[0]).results[0]["y_out"]
    return np.ascontiguousarray(y.transpose(1, 0, 4, 3, 2)).reshape(BATCHES, SEQ, C)
```
